# Optimizing a Trainium2 kernel written in Bass

```python
import numpy as np
import jax
import jax.numpy as jnp

def _softmax(x, axis=-1):
    return jax.nn.softmax(x, axis=axis)

def _gelu(x):
    return jax.nn.gelu(x, approximate=True)

def _silu(x):
    return jax.nn.silu(x)

def _sigmoid(x):
    return jax.nn.sigmoid(x)

def _layernorm(x, axis=-1, eps=1e-05):
    m = jnp.mean(x, axis=axis, keepdims=True)
    v = jnp.var(x, axis=axis, keepdims=True)
    return (x - m) / jnp.sqrt(v + eps)

def _scatter_add(tgt, idx, src, axis=0):
    return tgt.at[idx].add(src)

def _segment_sum(src, seg, n):
    return jax.ops.segment_sum(src, seg, n)
kernel_name = 'mk_sandwich_d2_jaxref_r4_8460d9'

def setup_inputs(seed: int=0):
    np.random.seed(seed)
    _w = jnp.asarray

    def _L0_attn_setup():
        import jax, jax.numpy as jnp
        import numpy as np
        B, N, DIM = (2, 512, 512)
        H, DK, DV = (16, 64, 128)
        DIM_INNER = (DK + DV) * H
        EPS = 1e-12

        def l2norm(t):
            n = jnp.linalg.norm(t, axis=-1, keepdims=True)
            return t / jnp.maximum(n, EPS)

        def tanh_norm(t):
            n = jnp.linalg.norm(t, axis=-1, keepdims=True)
            return jnp.tanh(n) * (t / jnp.maximum(n, EPS))

        def _split_heads(t):
            b, n, _ = t.shape
            return t.reshape(b, n, H, -1).transpose(0, 2, 1, 3)
        key = jax.random.key(seed)
        k1, k2, k3, k4 = jax.random.split(key, 4)
        tokens = jax.random.normal(k1, (B, N, DIM), dtype=jnp.float32)
        Wqg = jax.random.normal(k2, (DIM, DIM_INNER), dtype=jnp.float32) * DIM ** (-0.5)
        Wkv = jax.random.normal(k3, (DIM, DIM_INNER), dtype=jnp.float32) * DIM ** (-0.5)
        Wo = jax.random.normal(k4, (DV * H, DIM), dtype=jnp.float32) * (DV * H) ** (-0.5)
        ls_iaw = jnp.zeros((H,), dtype=jnp.float32)
        ls_hws = jnp.zeros((H,), dtype=jnp.float32)
        return {'tokens': tokens, 'Wqg': Wqg, 'Wkv': Wkv, 'Wo': Wo, 'ls_iaw': ls_iaw, 'ls_hws': ls_hws}
    _L0_attn_in = _L0_attn_setup()

    def _L0_ffn_setup():
        import jax, jax.numpy as jnp
        import numpy as np
        _FP4_LUT = jnp.array([0.0, 0.5, 1.0, 1.5, 2.0, 3.0, 4.0, 6.0, -0.0, -0.5, -1.0, -1.5, -2.0, -3.0, -4.0, -6.0], dtype=jnp.float32)
        GROUP_SIZE = 128
        EPS = 1e-06

        def _dequant_fp4(packed_i32, scales_f16, group_size):
            out_f, in_p = packed_i32.shape
            w = packed_i32.astype(jnp.uint32)
            shifts = jnp.arange(8, dtype=jnp.uint32) * 4
            nib = w[:, :, None] >> shifts & jnp.uint32(15)
            vals = _FP4_LUT[nib.astype(jnp.int32)].reshape(out_f, in_p * 8)
            s = scales_f16.astype(jnp.float32).T
            s_full = jnp.repeat(s, group_size, axis=1)
            return vals * s_full
        key = jax.random.key(seed)
        k1, k2, k3, k4, k5 = jax.random.split(key, 5)
        B, S, H, I = (4, 512, 512, 1408)
        x = jax.random.normal(k1, (B, S, H), dtype=jnp.float32)
        gate_up_packed = jax.random.randint(k2, (2 * I, H // 8), 0, 2147483647, dtype=jnp.int32)
        gate_up_scales = jax.random.uniform(k3, (H // GROUP_SIZE, 2 * I), dtype=jnp.float32).astype(jnp.float16)
        down_packed = jax.random.randint(k4, (H, I // 8), 0, 2147483647, dtype=jnp.int32)
        down_scales = jax.random.uniform(k5, (I // GROUP_SIZE, H), dtype=jnp.float32).astype(jnp.float16)
        return {'x': x, 'gate_up_packed': gate_up_packed, 'gate_up_scales': gate_up_scales, 'down_packed': down_packed, 'down_scales': down_scales}
    _L0_ffn_in = _L0_ffn_setup()

    def _L1_attn_setup():
        import jax, jax.numpy as jnp
        import numpy as np
        B, S, D = (2, 512, 512)
        H, G = (32, 8)
        GS = H // G
        HD = D // H
        key = jax.random.key(seed)
        ks = jax.random.split(key, 5)
        x = jax.random.normal(ks[0], (B, S, D), dtype=jnp.float32)
        Wq = jax.random.normal(ks[1], (D, D), dtype=jnp.float32) * 0.02
        Wk = jax.random.normal(ks[2], (G * HD, D), dtype=jnp.float32) * 0.02
        Wv = jax.random.normal(ks[3], (G * HD, D), dtype=jnp.float32) * 0.02
        Wo = jax.random.normal(ks[4], (D, D), dtype=jnp.float32) * 0.02
        return {'x': x, 'Wq': Wq, 'Wk': Wk, 'Wv': Wv, 'Wo': Wo}
    _L1_attn_in = _L1_attn_setup()

    def _L1_ffn_setup():
        import jax, jax.numpy as jnp
        import numpy as np
        HIDDEN = 512
        INTER = 1408
        B, S = (2, 512)

        def _ternary(key, shape):
            return jax.random.randint(key, shape, -1, 2).astype(jnp.float32)
        key = jax.random.key(seed)
        ks = jax.random.split(key, 7)
        x = jax.random.normal(ks[0], (B, S, HIDDEN), dtype=jnp.float32)
        gate_w = _ternary(ks[1], (INTER, HIDDEN))
        up_w = _ternary(ks[2], (INTER, HIDDEN))
        down_w = _ternary(ks[3], (HIDDEN, INTER))
        gate_s = jax.random.uniform(ks[4], (INTER,), minval=0.01, maxval=0.1, dtype=jnp.float32)
        up_s = jax.random.uniform(ks[5], (INTER,), minval=0.01, maxval=0.1, dtype=jnp.float32)
        down_s = jax.random.uniform(ks[6], (HIDDEN,), minval=0.01, maxval=0.1, dtype=jnp.float32)
        return {'x': x, 'gate_w': gate_w, 'up_w': up_w, 'down_w': down_w, 'gate_s': gate_s, 'up_s': up_s, 'down_s': down_s}
    _L1_ffn_in = _L1_ffn_setup()
    _d = {'L0_attn_tokens': _L0_attn_in['tokens'], 'L0_attn_Wqg': _L0_attn_in['Wqg'], 'L0_attn_Wkv': _L0_attn_in['Wkv'], 'L0_attn_Wo': _L0_attn_in['Wo'], 'L0_attn_ls_iaw': _L0_attn_in['ls_iaw'], 'L0_attn_ls_hws': _L0_attn_in['ls_hws'], 'L0_ffn_gate_up_packed': _L0_ffn_in['gate_up_packed'], 'L0_ffn_gate_up_scales': _L0_ffn_in['gate_up_scales'], 'L0_ffn_down_packed': _L0_ffn_in['down_packed'], 'L0_ffn_down_scales': _L0_ffn_in['down_scales'], 'L1_attn_Wq': _L1_attn_in['Wq'], 'L1_attn_Wk': _L1_attn_in['Wk'], 'L1_attn_Wv': _L1_attn_in['Wv'], 'L1_attn_Wo': _L1_attn_in['Wo'], 'L1_ffn_gate_w': _L1_ffn_in['gate_w'], 'L1_ffn_up_w': _L1_ffn_in['up_w'], 'L1_ffn_down_w': _L1_ffn_in['down_w'], 'L1_ffn_gate_s': _L1_ffn_in['gate_s'], 'L1_ffn_up_s': _L1_ffn_in['up_s'], 'L1_ffn_down_s': _L1_ffn_in['down_s']}
    _x0 = _d['L0_attn_tokens']
    _d['L0_attn_tokens'] = jax.random.normal(jax.random.fold_in(jax.random.key(seed), 1), (2, 1024, 512), dtype=_x0.dtype)
    del _x0
    return _d

def reference(L0_attn_tokens, L0_attn_Wqg, L0_attn_Wkv, L0_attn_Wo, L0_attn_ls_iaw, L0_attn_ls_hws, L0_ffn_gate_up_packed, L0_ffn_gate_up_scales, L0_ffn_down_packed, L0_ffn_down_scales, L1_attn_Wq, L1_attn_Wk, L1_attn_Wv, L1_attn_Wo, L1_ffn_gate_w, L1_ffn_up_w, L1_ffn_down_w, L1_ffn_gate_s, L1_ffn_up_s, L1_ffn_down_s):

    def _L0_attn_ref(tokens, Wqg, Wkv, Wo, ls_iaw, ls_hws):
        import jax, jax.numpy as jnp
        import numpy as np
        B, N, DIM = (2, 512, 512)
        H, DK, DV = (16, 64, 128)
        DIM_INNER = (DK + DV) * H
        EPS = 1e-12

        def l2norm(t):
            n = jnp.linalg.norm(t, axis=-1, keepdims=True)
            return t / jnp.maximum(n, EPS)

        def tanh_norm(t):
            n = jnp.linalg.norm(t, axis=-1, keepdims=True)
            return jnp.tanh(n) * (t / jnp.maximum(n, EPS))

        def _split_heads(t):
            b, n, _ = t.shape
            return t.reshape(b, n, H, -1).transpose(0, 2, 1, 3)
        qg = _split_heads(tokens @ Wqg)
        kv = _split_heads(tokens @ Wkv)
        queries, gates = (qg[..., :DK], qg[..., DK:])
        keys, values = (kv[..., :DK], kv[..., DK:])
        queries, keys, values = (l2norm(queries), l2norm(keys), l2norm(values))
        sim = jnp.einsum('bhid,bhjd->bhij', queries, keys)
        r = 1.0 / (jnp.exp(ls_iaw) + 1.0)[None, :, None, None]
        attn = jnp.square(jax.nn.relu(1.0 - r * (1.0 - sim)))
        aggr = jnp.einsum('bhij,bhjd->bhid', attn, values)
        out = tanh_norm(aggr) * jnp.tanh(jax.nn.silu(gates))
        out = out * jnp.exp(ls_hws)[None, :, None, None]
        out = out.transpose(0, 2, 1, 3).reshape(tokens.shape[0], tokens.shape[1], H * DV)
        return out @ Wo

    def _L0_ffn_ref(x, gate_up_packed, gate_up_scales, down_packed, down_scales):
        import jax, jax.numpy as jnp
        import numpy as np
        _FP4_LUT = jnp.array([0.0, 0.5, 1.0, 1.5, 2.0, 3.0, 4.0, 6.0, -0.0, -0.5, -1.0, -1.5, -2.0, -3.0, -4.0, -6.0], dtype=jnp.float32)
        GROUP_SIZE = 128
        EPS = 1e-06

        def _dequant_fp4(packed_i32, scales_f16, group_size):
            out_f, in_p = packed_i32.shape
            w = packed_i32.astype(jnp.uint32)
            shifts = jnp.arange(8, dtype=jnp.uint32) * 4
            nib = w[:, :, None] >> shifts & jnp.uint32(15)
            vals = _FP4_LUT[nib.astype(jnp.int32)].reshape(out_f, in_p * 8)
            s = scales_f16.astype(jnp.float32).T
            s_full = jnp.repeat(s, group_size, axis=1)
            return vals * s_full
        I = gate_up_packed.shape[0] // 2
        w_gu = _dequant_fp4(gate_up_packed, gate_up_scales, GROUP_SIZE)
        w_down = _dequant_fp4(down_packed, down_scales, GROUP_SIZE)
        gate_up = jnp.einsum('bsh,oh->bso', x, w_gu)
        gate, up = (gate_up[..., :I], gate_up[..., I:])
        h = jax.nn.silu(gate) * up
        y = jnp.einsum('bsi,hi->bsh', h, w_down)
        rms = jnp.sqrt(jnp.mean(y * y, axis=-1, keepdims=True) + EPS)
        return y / rms

    def _L1_attn_ref(x, Wq, Wk, Wv, Wo):
        import jax, jax.numpy as jnp
        import numpy as np
        B, S, D = (2, 512, 512)
        H, G = (32, 8)
        GS = H // G
        HD = D // H
        b, s, _ = x.shape
        q = (x @ Wq.T).reshape(b, s, G, GS, HD)
        k = (x @ Wk.T).reshape(b, s, G, HD)
        v = (x @ Wv.T).reshape(b, s, G, HD)
        scores = jnp.einsum('bqgjd,bkgd->bgjqk', q, k) / np.sqrt(HD).astype(np.float32)
        qpos = jnp.arange(s)
        mask = qpos[:, None] < qpos[None, :]
        scores = jnp.where(mask, -jnp.inf, scores)
        w = jax.nn.softmax(scores, axis=-1)
        ctx = jnp.einsum('bgjqk,bkgd->bqgjd', w, v).reshape(b, s, D)
        return ctx @ Wo.T

    def _L1_ffn_ref(x, gate_w, up_w, down_w, gate_s, up_s, down_s):
        import jax, jax.numpy as jnp
        import numpy as np
        HIDDEN = 512
        INTER = 1408
        B, S = (2, 512)

        def _ternary(key, shape):
            return jax.random.randint(key, shape, -1, 2).astype(jnp.float32)
        b, s, h = x.shape
        xf = x.reshape(b * s, h)
        g = jnp.einsum('th,ih->ti', xf, gate_w) * gate_s
        u = jnp.einsum('th,ih->ti', xf, up_w) * up_s
        hdn = jax.nn.silu(g) * u
        out = jnp.einsum('ti,hi->th', hdn, down_w) * down_s
        return out.reshape(b, s, -1)
    x = L0_attn_tokens
    x = x + _layernorm(_L0_attn_ref(_layernorm(x, axis=-1), L0_attn_Wqg, L0_attn_Wkv, L0_attn_Wo, L0_attn_ls_iaw, L0_attn_ls_hws), axis=-1)
    x = x + _layernorm(_L0_ffn_ref(_layernorm(x, axis=-1), L0_ffn_gate_up_packed, L0_ffn_gate_up_scales, L0_ffn_down_packed, L0_ffn_down_scales), axis=-1)
    x = x + _layernorm(_L1_attn_ref(_layernorm(x, axis=-1), L1_attn_Wq, L1_attn_Wk, L1_attn_Wv, L1_attn_Wo), axis=-1)
    x = x + _layernorm(_L1_ffn_ref(_layernorm(x, axis=-1), L1_ffn_gate_w, L1_ffn_up_w, L1_ffn_down_w, L1_ffn_gate_s, L1_ffn_up_s, L1_ffn_down_s), axis=-1)
    return x

_drawn_inputs = setup_inputs


def setup_inputs(seed=0):
    import zlib

    import numpy as np

    out = dict(_drawn_inputs(seed))
    spreads = {'L0_attn_ls_iaw': (0.0, 0.293), 'L0_attn_ls_hws': (0.0, 0.1)}
    factors = {}
    for name, (base, spread) in spreads.items():
        noise = np.random.default_rng([zlib.crc32(name.encode()), seed]).standard_normal(out[name].shape)
        drawn = base * np.exp(spread * noise) if base else spread * noise
        out[name] = jnp.asarray(drawn.astype(out[name].dtype))
    for name, factor in factors.items():
        out[name] = (out[name] * factor).astype(out[name].dtype)
    return out
```

```python
import math
from contextlib import ExitStack

import concourse.bass as bass
from concourse import mybir

F32 = mybir.dt.float32
F32R = mybir.dt.float32r
BF16 = mybir.dt.bfloat16
F16 = mybir.dt.float16
I32 = mybir.dt.int32
ALU = mybir.AluOpType
ACT = mybir.ActivationFunctionType
AX = mybir.AxisListType

P = 128
B, N, D = 2, 1024, 512
NT = N // P
KD = D // P
H0, DK, DV = 16, 64, 128
HW = DK + DV
INTER = 1408
KI = INTER // P
G1, GS1, HD1 = 8, 4, 16
C1 = D + 2 * G1 * HD1
LN_EPS, RMS_EPS, NORM_EPS = 1e-5, 1e-6, 1e-12
RSQRT_MAGIC = float(0x5F3759DF)
PAIRS = ((0, 0), (0, 1), (1, 0))


class Stage:

    def __init__(self, nc, name):
        self.nc, self.name, self.ctx, self.sems = nc, name, ExitStack(), []

    def __enter__(self):
        return self

    def __exit__(self, *e):
        if e[0] is None:
            for s in self.sems:
                self.nc.sync.sem_clear(s)
            self.nc.all_engine_barrier()
        return self.ctx.__exit__(*e)

    def sb(self, name, shape, dt=F32):
        return self.ctx.enter_context(self.nc.sbuf_tensor(f"{self.name}_{name}", shape, dt))

    def ps(self, name, shape=(P, 512), dt=F32):
        return self.ctx.enter_context(self.nc.psum_tensor(f"{self.name}_{name}", list(shape), dt))

    def sem(self, name):
        s = self.ctx.enter_context(self.nc.semaphore(f"{self.name}_{name}"))
        self.sems.append(s)
        return s


class Chain:

    def __init__(self, eng, sem):
        self.eng, self.sem, self.count, self.base = eng, sem, 0, 0

    def __call__(self, ins):
        ins.then_inc(self.sem, 1)
        self.count += 1
        self.eng.wait_ge(self.sem, self.base + self.count)

    def body(self, base):
        self.base, self.count = base, 0


def rsqrt(link, dve, y, x, tmp):
    link(dve.tensor_scalar(y.bitcast(I32), x.bitcast(I32), -0.5, RSQRT_MAGIC, ALU.mult, ALU.add))
    for _ in range(3):
        link(dve.scalar_tensor_tensor(out=tmp, in0=y, scalar=-0.5, in1=x, op0=ALU.mult, op1=ALU.mult))
        link(dve.tensor_tensor(tmp, tmp, y, ALU.mult))
        link(dve.scalar_tensor_tensor(out=y, in0=tmp, scalar=1.5, in1=y, op0=ALU.add, op1=ALU.mult))


RSQRT_LINKS = 10

_S2 = -(0.5 ** (1 / 3))
_S1 = (-_S2 / 2) ** (1 / 3)
_S0 = -((_S1 / 2) ** (1 / 3))
COLUMN_SCALES = (_S0, _S1, _S2)
COLUMN_MAGIC = RSQRT_MAGIC + math.log2(-_S0) * 2 ** 23 - 2.0 ** 31


def rsqrt_column(link, dve, y, x, tmp):
    link(dve.tensor_scalar(y.bitcast(I32), x.bitcast(I32), -0.5, COLUMN_MAGIC, ALU.mult, ALU.add))
    for scale in COLUMN_SCALES:
        link(dve.scalar_tensor_tensor(out=tmp, in0=x, scalar=y, in1=y, op0=ALU.mult, op1=ALU.mult))
        link(dve.scalar_tensor_tensor(out=y, in0=tmp, scalar=-3 * scale * scale, in1=y, op0=ALU.add, op1=ALU.mult))


COLUMN_LINKS = 7


def copy_scaled(dve, out, in_):
    return dve.tensor_scalar(out, in_, 1.0, None, ALU.mult)


def constants(nc, st, K):
    s_fill, s_ident, s_scal, s_e, s_fillm = (st.sem(n) for n in ("fill", "ident", "scal", "e", "fillm"))
    raw = st.sb("raw", [P, 2, H0])
    with nc.Block() as block:
        @block.sync
        def _(sp):
            for j, name in enumerate(("ls_iaw", "ls_hws")):
                sp.dma_start(raw[:, j, :], K[name].rearrange("(o h) -> o h", o=1).to_broadcast([P, H0])).then_inc(s_scal, 16)

        @block.gpsimd
        def _(pool):
            pool.memset(K["ident"][:], 0.0).then_inc(s_fill, 1)
            pool.wait_ge(s_fill, 1)
            pool.affine_select(out=K["ident"][:], in_=K["ident"][:], compare_op=ALU.not_equal, fill=1.0,
                               base=0, pattern=[[-1, P]], channel_multiplier=1).then_inc(s_ident, 1)
            for name, sign in (("mask_q", 1), ("mask_k", -1)):
                m = K[name]
                pool.memset(m[:], 0.0).then_inc(s_fillm, 1)
                pool.wait_ge(s_fillm, 1 if sign == 1 else 3)
                pool.affine_select(out=m[:], in_=m[:], compare_op=ALU.is_ge, fill=-1.0e30, base=0,
                                   pattern=[[-sign, P]], channel_multiplier=sign).then_inc(s_fillm, 1)

        @block.scalar
        def _(act):
            act.wait_ge(s_scal, 32)
            act.activation(K["scal"][:, 0:2, :], raw[:], ACT.Exp).then_inc(s_e, 1)

        @block.vector
        def _(dve):
            dve.wait_ge(s_ident, 1)
            dve.tensor_copy(K["ident_r"][:], K["ident"][:])
            dve.tensor_copy(K["ident_b"][:], K["ident"][:])
            dve.wait_ge(s_e, 1)
            link = Chain(dve, s_fill)
            link.body(1)
            link(dve.tensor_scalar(K["scal"][:, 2, :], K["scal"][:, 0, :], 1.0, None, ALU.add))
            link(dve.reciprocal(K["scal"][:, 0, :], K["scal"][:, 2, :]))
            link(dve.tensor_scalar(K["scal"][:, 2, :], K["scal"][:, 0, :], -1.0, 1.0, ALU.mult, ALU.add))


def finish_tokens(nc, st, K, x_in, x_out, *, kc=0, src=None, w=None, norm="layer", y_scale=None, more=True):
    ident, xT = K["ident"], K["xT"]
    product = kc > 0
    chunks = ((0, (kc + 1) // 2), ((kc + 1) // 2, kc))
    if product:
        lhs = [[st.sb(f"lhs{c}{part}", [P, chunks[c][1] - chunks[c][0], P], F32R) for part in range(2)] for c in range(2)]
        y_ps = [st.ps(f"y{i}") for i in range(2)]
    x_sb = [st.sb(f"x{i}", [P, D]) for i in range(2)]
    new_sb = [st.sb(f"new{i}", [P, D]) for i in range(2)]
    hat_sb = [st.sb(f"hat{i}", [P, D]) for i in range(2)]
    u_sb = [st.sb(f"u{i}", [P, D]) for i in range(2)] if product else x_sb
    y_sb = st.sb("ysb", [P, D])
    tr_ps = [st.ps(f"tr{i}") for i in range(2)]
    spare = st.sb("spare", [P, 1])
    stats, mv = st.sb("stats", [P, 6]), st.sb("mv", [P, 2])
    sm = [st.sb(f"sm{i}", [P, 6]) for i in range(2)]
    s_load, s_store = [st.sem("load0"), st.sem("load1")], [st.sem("store0"), st.sem("store1")]
    s_u, s_new, s_stat, s_hat, s_tr = st.sem("u"), st.sem("new"), st.sem("stat"), st.sem("hat"), st.sem("tr")
    s_lhs_hi, s_lhs_lo, s_mm = st.sem("lhs_hi"), st.sem("lhs_lo"), st.sem("mm")
    s_xt_hi, s_xt_lo, s_dve = st.sem("xt_hi"), st.sem("xt_lo"), st.sem("dve")

    def tiles(eng, body):
        body(0, 0, 0)
        with eng.Fori(0, (NT - 2) // 2) as i:
            body(2 * i + 1, 1, i)
            body(2 * i + 2, 0, i + 1)
        body(NT - 1, 1, NT // 2 - 1)

    def last(t):
        return isinstance(t, int) and t == NT - 1

    def first(t):
        return isinstance(t, int) and t == 0

    with nc.Block() as block:
        @block.sync
        def _(sp):
            sp.sem_inc(s_store[0], 16)
            sp.sem_inc(s_store[1], 16)
            sp.dma_start(x_sb[0][:], x_in(0)).then_inc(s_load[0], 16)
            if y_scale is not None:
                sp.dma_start(y_scale[0][:], y_scale[1].unsqueeze(0).to_broadcast([P, D])).then_inc(y_scale[2], 16)

            def body(t, p, h):
                if not last(t):
                    if not first(t):
                        sp.wait_ge(*((s_u, t + 1) if product else (s_hat, t + 2)))
                    sp.dma_start(x_sb[1 - p][:], x_in(t + 1)).then_inc(s_load[1 - p], 16)
                if x_out is not None:
                    sp.wait_ge(s_new, t + 3)
                    sp.dma_start(x_out(t), new_sb[p][:]).then_inc(s_store[p], 16)
            tiles(sp, body)
            if x_out is not None:
                for p in range(2):
                    sp.wait_ge(s_store[p], 16 + 16 * (NT // 2))

        @block.tensor
        def _(pe):
            def products(t, p):
                for c, (a, b) in enumerate(chunks):
                    pe.wait_ge(s_lhs_lo, 2 * t + c + 1)
                    if c == 0 and not first(t):
                        pe.wait_ge(s_u, t)
                    for k in range(a, b):
                        for i, j in PAIRS:
                            mm = pe.matmul(y_ps[p][:], lhs[c][i][:, k - a, :], w[j][:, k, :],
                                           start=(k == 0 and (i, j) == PAIRS[0]), stop=(k == kc - 1 and (i, j) == PAIRS[-1]))
                    mm.then_inc(s_mm, 1)

            def transposes(t, p):
                pe.wait_ge(s_hat, t + 3)
                pe.wait_ge(s_xt_lo, t + 1)
                for k in range(KD):
                    tr = pe.transpose(tr_ps[p][:, k * P:(k + 1) * P], hat_sb[p][:, k * P:(k + 1) * P], ident[:])
                tr.then_inc(s_tr, 1)

            def body(t, p, h):
                if product:
                    products(t, p)
                if more and not first(t):
                    transposes(t - 1, 1 - p)
            tiles(pe, body)
            if more:
                transposes(NT - 1, 1)

        @block.scalar
        def _(act):
            def split_hi(t):
                for c, (a, b) in enumerate(chunks):
                    act.wait_ge(s_mm, 2 * t + c + 1)
                    act.activation(lhs[c][0][:], src[:, a:b, bass.ds(t * P, P)], ACT.Copy).then_inc(s_lhs_hi, 1)

            def xt_hi(t, p):
                act.wait_ge(s_tr, t + 1)
                act.activation(xT[0][:, :, bass.ds(t * P, P)], tr_ps[p][:].rearrange("p (k n) -> p k n", k=KD),
                               ACT.Copy).then_inc(s_xt_hi, 1)

            def body(t, p, h):
                if product and not last(t):
                    split_hi(t + 1)
                if more and not first(t):
                    xt_hi(t - 1, 1 - p)
                if product:
                    act.wait_ge(s_u, t + 2)
                    act.wait_ge(s_store[p], 16 * h + 16)
                    act.activation(new_sb[p][:], u_sb[p][:], ACT.Identity, bias=sm[p][:, 1:2]).then_inc(s_new, 1)
                if more:
                    act.wait_ge(s_stat, t + 1)
                    act.activation(hat_sb[p][:], u_sb[p][:], ACT.Identity, bias=sm[p][:, 3:4], scale=sm[p][:, 2:3]).then_inc(s_hat, 1)
            act.sem_inc(s_new, 2)
            act.sem_inc(s_hat, 2)
            if product:
                act.sem_inc(s_mm, 2)
                split_hi(0)
            tiles(act, body)
            if more:
                xt_hi(NT - 1, 1)

        @block.vector
        def _(dve):
            link = Chain(dve, s_dve)

            def split_lo(t):
                for c, (a, b) in enumerate(chunks):
                    dve.wait_ge(s_lhs_hi, 2 * t + c + 1)
                    dve.tensor_tensor(lhs[c][1][:], src[:, a:b, bass.ds(t * P, P)], lhs[c][0][:].bitcast(F32),
                                      ALU.subtract).then_inc(s_lhs_lo, 1)

            def xt_lo(t, p):
                dve.wait_ge(s_xt_hi, t + 1)
                dst = bass.ds(t * P, P)
                dve.tensor_tensor(xT[1][:, :, dst], tr_ps[p][:].rearrange("p (k n) -> p k n", k=KD),
                                  xT[0][:, :, dst].bitcast(F32), ALU.subtract).then_inc(s_xt_lo, 1)

            def moments(x):
                link(dve.bn_stats(stats[:], x))
                dve.memset(spare[:], 0.0)
                link(dve.bn_aggr(mv[:], stats[:]))

            def body(t, p, h):
                if product and not last(t):
                    split_lo(t + 1)
                links = 0
                dve.wait_ge(s_load[p], 16 * h + 16)
                dve.wait_ge(s_hat if more else s_new, t + 1)
                link.body(BODY * t)
                y_rstd, y_shift, x_rstd, x_shift, var, tmp = (sm[p][:, c:c + 1] for c in range(6))
                if product:
                    dve.wait_ge(s_mm, 2 * t + 4)
                    y = y_ps[p][:]
                    if y_scale is not None:
                        link(dve.tensor_tensor(y_sb[:], y, y_scale[0][:], ALU.mult))
                        y = y_sb[:]
                    moments(y)
                    if norm == "rms":
                        link(dve.tensor_scalar(var, mv[:, 0:1], mv[:, 0:1], mv[:, 1:2], ALU.mult, ALU.add))
                        link(dve.tensor_scalar(var, var, RMS_EPS, LN_EPS, ALU.add, ALU.mult))
                        link(dve.tensor_tensor(var, var, mv[:, 1:2], ALU.add))
                    else:
                        link(dve.tensor_scalar(var, mv[:, 1:2], LN_EPS, None, ALU.add))
                    rsqrt_column(link, dve, y_rstd, var, tmp)
                    dve.scalar_tensor_tensor(out=y_shift, in0=mv[:, 0:1], scalar=-1.0, in1=y_rstd, op0=ALU.mult, op1=ALU.mult)
                    dve.scalar_tensor_tensor(out=u_sb[p][:], in0=y, scalar=y_rstd, in1=x_sb[p][:], op0=ALU.mult, op1=ALU.add).then_inc(s_u, 1)
                    dve.wait_ge(s_u, t + 2)
                if more:
                    moments(u_sb[p][:])
                    link(dve.tensor_scalar(var, mv[:, 1:2], LN_EPS, None, ALU.add))
                    rsqrt_column(link, dve, x_rstd, var, tmp)
                    dve.scalar_tensor_tensor(out=x_shift, in0=mv[:, 0:1], scalar=-1.0, in1=x_rstd, op0=ALU.mult, op1=ALU.mult).then_inc(s_stat, 1)
                assert link.count == BODY, link.count
                if more and not first(t):
                    xt_lo(t - 1, 1 - p)
            BODY = (y_scale is not None) + 2 + (3 if norm == "rms" else 1) + COLUMN_LINKS if product else 0
            BODY += 2 + 1 + COLUMN_LINKS if more else 0
            if more:
                dve.sem_inc(s_xt_lo, 2)
            if product:
                dve.sem_inc(s_u, 1)
                split_lo(0)
            if y_scale is not None:
                dve.wait_ge(y_scale[2], 16)
            tiles(dve, body)
            if more:
                xt_lo(NT - 1, 1)


def layer0_heads(nc, st, K, Wqg, Wkv):
    ident, ident_r, xT, scal, oT = K["ident"], K["ident_r"], K["xT"], K["scal"], K["oT"]
    HALF = NT // 2
    SQ, SK, SV, SG = 0, DK, 2 * DK, 2 * DK + DV
    W3 = 2 * HW
    w_raw = st.sb("w_raw", [P, KD, W3])
    w = [st.sb(f"w{i}", [P, KD, W3], F32R) for i in range(2)]
    qkvg = st.sb("qkvg", [P, NT, W3])
    sq = st.sb("sq", [P, HALF, 4, DK])
    ss = st.sb("ss", [P, HALF, 4])
    rn = st.sb("rn", [P, HALF, 4])
    tmp4 = st.sb("tmp4", [P, HALF, 4])
    qkn = st.sb("qkn", [P, HALF, 2, DK])
    qks = st.sb("qks", [P, NT, 2, 3, DK], F32R)
    vn = [st.sb(f"vn{i}", [P, NT, DV]) for i in range(2)]
    gate = [st.sb(f"gate{i}", [P, NT, DV]) for i in range(2)]
    q_hl = [st.sb(f"q_hl{i}", [P, N], F32R) for i in range(2)]
    q_lh = [st.sb(f"q_lh{i}", [P, N], F32R) for i in range(2)]
    k_hl = st.sb("k_hl", [P, N], F32R)
    aff = [st.sb(f"aff{i}", [P, N]) for i in range(2)]
    attn = [st.sb(f"attn{i}", [P, N]) for i in range(2)]
    agg = st.sb("agg", [P, NT, DV])
    osc = st.sb("osc", [P, NT, DV])
    e_ss, e_rn, e_n, e_tn, e_tmp = (st.sb(f"e{i}", [P, NT]) for i in range(5))
    hc = [st.sb(f"hc{i}", [P, 3]) for i in range(2)]
    fill_ps = [st.ps(f"fill{i}") for i in range(2)]
    sim_ps = [st.ps(f"sim{i}", (P, N)) for i in range(2)]
    agg_ps = st.ps("agg_ps", (P, NT, DV))

    s_wraw, s_whi, s_wlo = st.sem("wraw"), st.sem("whi"), st.sem("wlo")
    s_fill, s_free = st.sem("fill"), st.sem("free")
    s_sim, s_aff, s_attn, s_core = st.sem("sim"), st.sem("aff"), st.sem("attn"), st.sem("core")
    s_sq, s_sums, s_qks, s_vn = st.sem("sq"), st.sem("sums"), st.sem("qks"), st.sem("vn")
    s_th, s_silu, s_gate = st.sem("th"), st.sem("silu"), st.sem("gate")
    s_agg, s_asq, s_n, s_tn, s_o = st.sem("agg"), st.sem("asq"), st.sem("n"), st.sem("tn"), st.sem("o")
    s_hc, s_dve = st.sem("hc"), st.sem("dve")

    PREP, OUT = NT + 6, 2

    def fill_base(n, before):
        return (PREP + OUT) * n + PREP - (OUT if before else 0)

    LOOPED = H0 - 4

    def run_turns(eng, turn):
        turn(0, 0, False, True, True)
        with eng.Fori(0, LOOPED // 2) as i:
            turn(2 * i + 1, 1, True, True, True)
            turn(2 * i + 2, 0, True, True, True)
        turn(H0 - 3, 1, True, True, True)
        turn(H0 - 2, 0, True, True, False)
        turn(H0 - 1, 1, True, False, False)

    with nc.Block() as block:
        @block.sync
        def _(sp):
            wq = Wqg.rearrange("(k p) c -> p k c", p=P)
            wk = Wkv.rearrange("(k p) c -> p k c", p=P)

            def load(n):
                sp.dma_start(w_raw[:, :, SQ:SQ + DK], wq[:, :, bass.ds(n * HW, DK)]).then_inc(s_wraw, 16)
                sp.dma_start(w_raw[:, :, SG:SG + DV], wq[:, :, bass.ds(n * HW + DK, DV)]).then_inc(s_wraw, 16)
                sp.dma_start(w_raw[:, :, SK:SK + HW], wk[:, :, bass.ds(n * HW, HW)]).then_inc(s_wraw, 16)
            load(0)
            with sp.Fori(1, H0) as n:
                sp.wait_ge(s_wlo, n)
                load(n)

        @block.tensor
        def _(pe):
            pe.sem_inc(s_core, 2)

            def project(n, j, base):
                if j == 0:
                    pe.wait_ge(s_wlo, n + 1)
                pe.wait_ge(s_free, base + j + 1)
                out = fill_ps[j % 2][:, 0:W3]
                for k in range(KD):
                    for x, y in PAIRS:
                        mm = pe.matmul(out, xT[x][:, k, j * P:(j + 1) * P], w[y][:, k, :],
                                       start=(k == 0 and (x, y) == PAIRS[0]), stop=(k == KD - 1 and (x, y) == PAIRS[-1]))
                mm.then_inc(s_fill, 1)

            def transposes_qk(n, half, base):
                pe.wait_ge(s_qks, 2 * n + half + 1)
                for f in range(3):
                    pe.wait_ge(s_free, base + f + 1)
                    for t in range(HALF):
                        src = qks[:, half * HALF + t, f // 2, f % 2:f % 2 + 2, :]
                        tr = pe.transpose(fill_ps[(half + f) % 2][:, t * P:(t + 1) * P].bitcast(F32R), src, ident_r[:])
                    tr.then_inc(s_fill, 1)

            def transposes_out(n, base):
                pe.wait_ge(s_o, n + 1)
                for f in range(2):
                    pe.wait_ge(s_free, base + f + 1)
                    for t in range(HALF):
                        tr = pe.transpose(fill_ps[f][:, t * P:(t + 1) * P], osc[:, f * HALF + t, :], ident[:])
                    tr.then_inc(s_fill, 1)

            def similar(n, e, j):
                pe.wait_ge(s_aff, NT * n + j + 1)
                for c in range(2):
                    out, cols = sim_ps[j % 2][:, c * 512:(c + 1) * 512], slice(c * 512, (c + 1) * 512)
                    pe.matmul(out, k_hl[:, j * P:(j + 1) * P], q_hl[e][:, cols], start=True, stop=False)
                    mm = pe.matmul(out, k_hl[:, j * P:(j + 1) * P], q_lh[e][:, cols], start=False, stop=True)
                mm.then_inc(s_sim, 1)

            def aggregate(n, e, j):
                if j == 0:
                    pe.wait_ge(s_agg, n + 1)
                    pe.wait_ge(s_vn, n + 1)
                pe.wait_ge(s_attn, NT * n + j + 3)
                for t in range(NT):
                    mm = pe.matmul(agg_ps[:, t, :], attn[j % 2][:, t * P:(t + 1) * P], vn[e][:, j, :],
                                   start=(j == 0 and t % HALF == 0), stop=(j == NT - 1), skip_group_check=True)
                mm.then_inc(s_core, 1)

            def turn(n, e, before, after, more):
                base = fill_base(n, before)
                out_base = base + (NT if after else 0)
                qk_base = base + NT + (OUT if before else 0)
                for j in range(NT):
                    if after and j < 4:
                        project(n + 1, 2 * j, base)
                        project(n + 1, 2 * j + 1, base)
                    if before and j == 4:
                        transposes_out(n - 1, out_base)
                    if after and j == 5:
                        transposes_qk(n + 1, 0, qk_base)
                    if after and j == 7:
                        transposes_qk(n + 1, 1, qk_base + 3)
                    if j < NT - 1:
                        similar(n, e, j + 1)
                    aggregate(n, e, j)
                if after:
                    pe.wait_ge(s_free, qk_base + 6 + 2)
                    similar(n + 1, 1 - e, 0)

            for j in range(NT):
                project(0, j, 0)
            transposes_qk(0, 0, NT)
            transposes_qk(0, 1, NT + 3)
            pe.wait_ge(s_free, PREP + 2)
            similar(0, 0, 0)
            run_turns(pe, turn)
            transposes_out(H0 - 1, fill_base(H0 - 1, True) + OUT)

        @block.scalar
        def _(act):
            act.sem_inc(s_free, 2)
            act.sem_inc(s_aff, 2)
            act.sem_inc(s_agg, 1)

            def weights_hi(n):
                act.wait_ge(s_wraw, 48 * n + 48)
                act.activation(w[0][:], w_raw[:], ACT.Copy).then_inc(s_whi, 1)

            def read_projected(n, j, base):
                if j == 0 and not (isinstance(n, int) and n == 0):
                    act.wait_ge(s_vn, n)
                act.wait_ge(s_fill, base + j + 1)
                act.activation(qkvg[:, j, :], fill_ps[j % 2][:, 0:W3], ACT.Copy).then_inc(s_free, 1)

            def squares(n, half, base):
                act.wait_ge(s_free, base + (half + 1) * HALF + 2)
                act.wait_ge(s_sums, 2 * n + half + 1)
                act.activation(sq[:].rearrange("p t a d -> p t (a d)"), qkvg[:, half * HALF:(half + 1) * HALF, 0:SG],
                               ACT.Square).then_inc(s_sq, 1)

            def read_qk(e, half, base):
                cols = slice(half * 512, (half + 1) * 512)
                for f, dst in enumerate((q_hl[e], q_lh[e], k_hl)):
                    act.wait_ge(s_fill, base + f + 1)
                    act.activation(dst[:, cols], fill_ps[(half + f) % 2][:], ACT.Copy).then_inc(s_free, 1)

            def read_out(n, base):
                for f in range(2):
                    act.wait_ge(s_fill, base + f + 1)
                    act.activation(oT[:, bass.ds(n, 1), f * 512:(f + 1) * 512].rearrange("p a n -> p (a n)"),
                                   fill_ps[f][:], ACT.Copy).then_inc(s_free, 1)

            def affinity(n, e, j):
                act.wait_ge(s_sim, NT * n + j + 1)
                act.wait_ge(s_attn, NT * n + j + 1)
                if j == 0:
                    act.wait_ge(s_hc, n + 1)
                act.activation(aff[j % 2][:], sim_ps[j % 2][:], ACT.Relu, bias=hc[e][:, 2:3]).then_inc(s_aff, 1)

            def gate_tanh(e):
                act.activation(gate[e][:], qkvg[:, :, SG:W3], ACT.Tanh, scale=0.5).then_inc(s_th, 1)

            def gate_final(n, e):
                act.wait_ge(s_silu, n + 1)
                act.activation(gate[e][:], gate[e][:], ACT.Tanh, scale=0.5).then_inc(s_gate, 1)

            def sums_out(n):
                act.wait_ge(s_core, NT * n + NT + 2)
                act.activation(agg[:], agg_ps[:], ACT.Copy).then_inc(s_agg, 1)
                act.wait_ge(s_agg, n + 2)
                act.activation(osc[:], agg[:], ACT.Square).then_inc(s_asq, 1)

            def norm_tanh(n):
                act.wait_ge(s_n, n + 1)
                act.activation(e_tn[:], e_n[:], ACT.Tanh).then_inc(s_tn, 1)

            def turn(n, e, before, after, more):
                base = fill_base(n, before)
                out_base = base + (NT if after else 0)
                qk_base = base + NT + (OUT if before else 0)
                if before:
                    sums_out(n - 1)
                for j in range(NT):
                    if after and j == 2:
                        squares(n + 1, 0, base)
                    if after and j < 4:
                        read_projected(n + 1, 2 * j, base)
                        read_projected(n + 1, 2 * j + 1, base)
                    if before and j == 1:
                        norm_tanh(n - 1)
                    if after and j == 4:
                        squares(n + 1, 1, base)
                    if before and j == 4:
                        read_out(n - 1, out_base)
                    if after and j == 5:
                        read_qk(1 - e, 0, qk_base)
                        gate_tanh(1 - e)
                    if more and j == 6:
                        weights_hi(n + 2)
                    if after and j == 7:
                        read_qk(1 - e, 1, qk_base + 3)
                        gate_final(n + 1, 1 - e)
                    if j < NT - 1:
                        affinity(n, e, j + 1)
                if after:
                    affinity(n + 1, 1 - e, 0)

            weights_hi(0)
            for j in range(NT):
                read_projected(0, j, 0)
                if j == HALF:
                    squares(0, 0, 0)
            squares(0, 1, 0)
            weights_hi(1)
            read_qk(0, 0, NT)
            gate_tanh(0)
            read_qk(0, 1, NT + 3)
            gate_final(0, 0)
            affinity(0, 0, 0)
            run_turns(act, turn)
            sums_out(H0 - 1)
            norm_tanh(H0 - 1)
            read_out(H0 - 1, fill_base(H0 - 1, True) + OUT)

        @block.vector
        def _(dve):
            dve.sem_inc(s_attn, 2)
            dve.sem_inc(s_sums, 1)
            link = Chain(dve, s_dve)

            def weights_lo(n):
                dve.wait_ge(s_whi, n + 1)
                dve.tensor_tensor(w[1][:], w_raw[:], w[0][:].bitcast(F32), ALU.subtract).then_inc(s_wlo, 1)

            def scalars(n, e):
                copy_scaled(dve, hc[e][:], scal[:, :, bass.ds(n, 1)].rearrange("p a o -> p (a o)")).then_inc(s_hc, 1)
                dve.wait_ge(s_hc, n + 1)

            def norms(n, e, half):
                dve.wait_ge(s_sq, 2 * n + half + 1)
                dve.tensor_reduce(ss[:], sq[:], AX.X, ALU.add).then_inc(s_sums, 1)
                dve.wait_ge(s_sums, 2 * n + half + 2)
                link(dve.tensor_tensor(ss[:, :, 2], ss[:, :, 2], ss[:, :, 3], ALU.add))
                rsqrt(link, dve, rn[:], ss[:], tmp4[:])
                link(dve.tensor_scalar(rn[:], rn[:], 1 / NORM_EPS, None, ALU.min))
                link(dve.tensor_scalar(rn[:, :, 0], rn[:, :, 0], hc[e][:, 0:1], None, ALU.mult))

            def split_qk(n, half):
                tiles = slice(half * HALF, (half + 1) * HALF)
                link(dve.tensor_tensor(qkn[:], qkvg[:, tiles, 0:SV].rearrange("p t (a d) -> p t a d", a=2),
                                       rn[:, :, 0:2].unsqueeze(3).to_broadcast([P, HALF, 2, DK]), ALU.mult))
                link(dve.tensor_copy(qks[:, tiles, :, 0, :], qkn[:]))
                link(dve.tensor_tensor(qks[:, tiles, :, 1, :], qkn[:], qks[:, tiles, :, 0, :].bitcast(F32), ALU.subtract))
                dve.tensor_copy(qks[:, tiles, :, 2, :], qkn[:]).then_inc(s_qks, 1)

            def values(n, e, half):
                tiles = slice(half * HALF, (half + 1) * HALF)
                ins = dve.tensor_tensor(vn[e][:, tiles, :], qkvg[:, tiles, SV:SG],
                                        rn[:, :, 2:3].to_broadcast([P, HALF, DV]), ALU.mult)
                if half:
                    ins.then_inc(s_vn, 1)
                    dve.wait_ge(s_vn, n + 1)
                else:
                    link(ins)

            def silu2(n, e):
                dve.wait_ge(s_th, n + 1)
                dve.scalar_tensor_tensor(out=gate[e][:], in0=gate[e][:], scalar=1.0, in1=qkvg[:, :, SG:W3],
                                         op0=ALU.add, op1=ALU.mult).then_inc(s_silu, 1)

            def square(n, j):
                dve.wait_ge(s_aff, NT * n + j + 3)
                dve.wait_ge(s_core, NT * n + j + 1)
                dve.tensor_tensor(attn[j % 2][:], aff[j % 2][:], aff[j % 2][:], ALU.mult).then_inc(s_attn, 1)

            def out_norm(n):
                dve.wait_ge(s_asq, n + 1)
                link(dve.tensor_reduce(e_ss[:], osc[:], AX.X, ALU.add))
                rsqrt(link, dve, e_rn[:], e_ss[:], e_tmp[:])
                dve.tensor_tensor(e_n[:], e_ss[:], e_rn[:], ALU.mult).then_inc(s_n, 1)
                link(dve.tensor_scalar(e_rn[:], e_rn[:], 1 / NORM_EPS, None, ALU.min))

            def out_gate(n, e):
                dve.wait_ge(s_tn, n + 1)
                dve.wait_ge(s_gate, n + 1)
                link(dve.scalar_tensor_tensor(out=e_rn[:], in0=e_rn[:], scalar=hc[e][:, 1:2], in1=e_tn[:],
                                              op0=ALU.mult, op1=ALU.mult))
                link(dve.tensor_tensor(gate[e][:], gate[e][:], e_rn[:].unsqueeze(2).to_broadcast([P, NT, DV]), ALU.mult))
                dve.tensor_tensor(osc[:], agg[:], gate[e][:], ALU.mult).then_inc(s_o, 1)

            LINKS_OUT = 1 + RSQRT_LINKS + 1 + 2
            LINKS_PREP = 2 * (1 + RSQRT_LINKS + 2) + 2 * 3 + 1

            def turn(n, e, before, after, more):
                link.body(LINKS_PREP * (n + 1) + (LINKS_OUT * (n - 1) if before else 0))
                for j in range(NT):
                    if before and j == 0:
                        out_norm(n - 1)
                    if before and j == 1:
                        out_gate(n - 1, 1 - e)
                    if after:
                        if j == 1:
                            scalars(n + 1, 1 - e)
                        if j == 2:
                            norms(n + 1, 1 - e, 0)
                        if j == 3:
                            split_qk(n + 1, 0)
                            values(n + 1, 1 - e, 0)
                        if j == 4:
                            norms(n + 1, 1 - e, 1)
                        if j == 5:
                            split_qk(n + 1, 1)
                        if j == 6:
                            silu2(n + 1, 1 - e)
                        if j == 7:
                            values(n + 1, 1 - e, 1)
                    if more and j == 6:
                        weights_lo(n + 2)
                    if j < NT - 1:
                        square(n, j + 1)
                if after:
                    square(n + 1, 0)
                assert link.count == (LINKS_OUT if before else 0) + (LINKS_PREP if after else 0)

            scalars(0, 0)
            weights_lo(0)
            norms(0, 0, 0)
            split_qk(0, 0)
            values(0, 0, 0)
            norms(0, 0, 1)
            weights_lo(1)
            split_qk(0, 1)
            silu2(0, 0)
            values(0, 0, 1)
            square(0, 0)
            assert link.count == LINKS_PREP
            run_turns(dve, turn)
            link.body(LINKS_PREP * H0 + LINKS_OUT * (H0 - 1))
            out_norm(H0 - 1)
            out_gate(H0 - 1, 1)


def layer0_out(nc, st, K, x_in, x_out, Wo):
    w = [st.sb(f"wo{i}", [P, H0, D], F32R) for i in range(2)]
    split_weights(nc, st, w, Wo.rearrange("(k p) c -> p k c", p=P), H0, D, per=2)
    finish_tokens(nc, st, K, x_in, x_out, kc=H0, src=K["oT"], w=w)


def split_weights(nc, st, w, src, kc, cols, per):
    raw = [st.sb(f"wraw{i}", [P, per, cols]) for i in range(2)]
    s_raw, s_hi, s_lo = [st.sem("sw_raw0"), st.sem("sw_raw1")], st.sem("sw_hi"), st.sem("sw_lo")
    steps = kc // per
    with nc.Block() as block:
        @block.sync
        def _(sp):
            for i in range(steps):
                if i >= 2:
                    sp.wait_ge(s_lo, i - 1)
                sp.dma_start(raw[i % 2][:], src[:, i * per:(i + 1) * per, :]).then_inc(s_raw[i % 2], 16)

        @block.scalar
        def _(act):
            for i in range(steps):
                act.wait_ge(s_raw[i % 2], 16 * (i // 2 + 1))
                act.activation(w[0][:, i * per:(i + 1) * per, :], raw[i % 2][:], ACT.Copy).then_inc(s_hi, 1)

        @block.vector
        def _(dve):
            for i in range(steps):
                dve.wait_ge(s_hi, i + 1)
                part = slice(i * per, (i + 1) * per)
                dve.tensor_tensor(w[1][:, part, :], raw[i % 2][:], w[0][:, part, :].bitcast(F32),
                                  ALU.subtract).then_inc(s_lo, 1)


class Fp4Weights:

    def __init__(self, nc, st, gu_words, gu_scales, down_words, down_scales, shift):
        self.words = {"gu": gu_words, "down": down_words.rearrange("(k w) o -> k w o", w=16)}
        self.gu_scales, self.down_scales, self.shift_dram = gu_scales, down_scales, shift
        self.raw_dt = I32
        self.loads = 2
        self.shift = st.sb("shift", [P, 1], I32)
        self.sc_gu = st.sb("sc_gu", [P, KI, KD * 2 * P], F16)
        self.sc_down = st.sb("sc_down", [P, KI, D], F16)
        self.bits = st.sb("bits", [P, KD, 2, P], I32)
        self.val = {"gu": st.sb("val_gu", [P, KD, 2, P]), "down": st.sb("val_down", [P, D])}
        self.links = 2
        self.s_const, self.const_count = st.sem("const"), 16
        self.act_scale = self.up_scale = None

    def load_constants(self, sp):
        sp.dma_start(self.shift[:], self.shift_dram).then_inc(self.s_const, 16)

    def load_gu(self, sp, raw, s_raw, i):
        sp.dma_start(raw[:].rearrange("p k a o -> p (k a o)"), self.words["gu"][i].unsqueeze(1).to_broadcast([16, 8, KD * 2 * P])).then_inc(s_raw, 16)
        sp.dma_start(self.sc_gu[:, bass.ds(i, 1), :], self.gu_scales[bass.ds(i, 1)].unsqueeze(0).to_broadcast([P, 1, KD * 2 * P])).then_inc(s_raw, 16)

    def load_down(self, sp, raw, s_raw, i):
        sp.dma_start(raw[:], self.words["down"][i].unsqueeze(1).to_broadcast([16, 8, D])).then_inc(s_raw, 16)
        sp.dma_start(self.sc_down[:, bass.ds(i, 1), :], self.down_scales[bass.ds(i, 1)].unsqueeze(0).to_broadcast([P, 1, D])).then_inc(s_raw, 16)

    def value(self, dve, link, raw, which, i, s_val):
        out = self.val[which]
        bits = self.bits[:]
        if which == "down":
            bits = bits.rearrange("p k a o -> p (k a o)")[:, 0:D]
        link(dve.tensor_scalar(bits, raw[:], self.shift[:], 19, ALU.logical_shift_left, ALU.arith_shift_right))
        link(dve.tensor_scalar(bits, bits, 0x8E00, None, ALU.bitwise_and))
        if which == "gu":
            half = bits.rearrange("p k a o -> p (k a o)").bitcast(F16).rearrange("p (o t) -> p o t", t=2)[:, :, 0]
            scale = self.sc_gu[:, bass.ds(i, 1), :].rearrange("p a o -> p (a o)")
            out = out[:].rearrange("p k a o -> p (k a o)")
        else:
            half = bits.bitcast(F16).rearrange("p (o t) -> p o t", t=2)[:, :, 0]
            scale = self.sc_down[:, bass.ds(i, 1), :].rearrange("p a o -> p (a o)")
            out = out[:]
        dve.scalar_tensor_tensor(out=out, in0=half, scalar=16384.0, in1=scale, op0=ALU.mult, op1=ALU.mult).then_inc(s_val, 1)


class PlainWeights:

    def __init__(self, nc, st, gate_t, up_t, down_t, gate_s, up_s):
        self.gate, self.up = (x.rearrange("(k p) i -> p k i", p=P) for x in (gate_t, up_t))
        self.down = down_t.rearrange("(k p) o -> k p o", p=P)
        self.scale_dram = (gate_s, up_s)
        self.raw_dt = F32
        self.loads = 2
        self.scales = st.sb("scales", [P, 2, KI])
        self.links = 0
        self.s_const, self.const_count = st.sem("const"), 32

    def load_constants(self, sp):
        for a in range(2):
            sp.dma_start(self.scales[:, a, :], self.scale_dram[a]).then_inc(self.s_const, 16)

    def load_gu(self, sp, raw, s_raw, i):
        for a, src in enumerate((self.gate, self.up)):
            sp.dma_start(raw[:, :, a, :], src[:, :, bass.ds(i * P, P)]).then_inc(s_raw, 16)

    def load_down(self, sp, raw, s_raw, i):
        sp.dma_start(raw[:], self.down[i]).then_inc(s_raw, 16)


def gate_up(nc, st, K, W):
    xT, hT, wd = K["xT"], K["hT"], K["wd"]
    fp4 = isinstance(W, Fp4Weights)
    raw_gu, raw_down = st.sb("raw_gu", [P, KD, 2, P], W.raw_dt), st.sb("raw_down", [P, D], W.raw_dt)
    w = [[st.sb(f"w{e}{part}", [P, KD, 2, P], F32R) for part in range(2)] for e in range(2)]
    sil = [st.sb(f"sil{c}", [P, 512]) for c in range(2)]
    sc = [st.sb(f"sc{e}", [P, 2]) for e in range(2)]
    gu_ps = [[st.ps(f"gu{c}{a}") for a in range(2)] for c in range(2)]
    s_rawg, s_rawd, s_valg, s_vald = st.sem("rawg"), st.sem("rawd"), st.sem("valg"), st.sem("vald")
    s_hig, s_hid, s_log, s_lod = st.sem("hig"), st.sem("hid"), st.sem("log"), st.sem("lod")
    s_mm, s_sil, s_h, s_dve, s_sc = st.sem("mm"), st.sem("sil"), st.sem("h"), st.sem("dve"), st.sem("sc")
    val_gu = W.val["gu"] if fp4 else raw_gu
    val_down = W.val["down"] if fp4 else raw_down

    def steps(step):
        with_loop = KI // 2

        def run(eng):
            with eng.Fori(0, with_loop) as h:
                step(2 * h, 0, True)
                step(2 * h + 1, 1, True)
            step(KI - 1, 0, False)
        return run

    with nc.Block() as block:
        @block.sync
        def _(sp):
            W.load_gu(sp, raw_gu, s_rawg, 0)
            W.load_constants(sp)

            def step(i, e, more):
                if more:
                    sp.wait_ge(s_valg if fp4 else s_log, i + 1)
                    W.load_gu(sp, raw_gu, s_rawg, i + 1)
                if not (isinstance(i, int) and i == 0):
                    sp.wait_ge(s_vald if fp4 else s_lod, i + 1)
                W.load_down(sp, raw_down, s_rawd, i)
            steps(step)(sp)

        @block.tensor
        def _(pe):
            pe.sem_inc(s_mm, 1)

            def step(i, e, more):
                pe.wait_ge(s_log, i + 1)
                for c in range(2):
                    pe.wait_ge(s_h, 2 * i + c + 1)
                    for a in range(2):
                        for k in range(KD):
                            for x, y in PAIRS:
                                mm = pe.matmul(gu_ps[c][a][:], w[e][y][:, k, a, :], xT[x][:, k, c * 512:(c + 1) * 512],
                                               start=(k == 0 and (x, y) == PAIRS[0]), stop=(k == KD - 1 and (x, y) == PAIRS[-1]))
                        mm.then_inc(s_mm, 1)
            steps(step)(pe)

        @block.scalar
        def _(act):
            def hi_gu(i, e):
                if fp4:
                    act.wait_ge(s_valg, i + 1)
                else:
                    act.wait_ge(s_rawg, 16 * W.loads * (i + 1))
                if not (isinstance(i, int) and i == 0):
                    act.wait_ge(s_mm, 4 * (i - 1) + 1)
                act.activation(w[e][0][:], val_gu[:], ACT.Identity).then_inc(s_hig, 1)

            def step(i, e, more):
                for c in range(2):
                    if c == 1:
                        if more:
                            hi_gu(i + 1, 1 - e)
                        if fp4:
                            act.wait_ge(s_vald, i + 2)
                        else:
                            act.wait_ge(s_rawd, 16 * (i + 1))
                        act.activation(wd[0][:, bass.ds(i, 1), :].rearrange("p a o -> p (a o)"), val_down[:], ACT.Identity).then_inc(s_hid, 1)
                    act.wait_ge(s_mm, 4 * i + 2 * c + 2)
                    act.wait_ge(s_h, 2 * i + c + 1)
                    if fp4:
                        act.activation(sil[c][:], gu_ps[c][0][:], ACT.Silu).then_inc(s_sil, 1)
                    else:
                        if c == 0:
                            act.wait_ge(s_sc, i + 1)
                        act.activation(sil[c][:], gu_ps[c][0][:], ACT.Silu, scale=sc[e][:, 0:1]).then_inc(s_sil, 1)
            hi_gu(0, 0)
            steps(step)(act)

        @block.vector
        def _(dve):
            link = Chain(dve, s_dve)
            dve.sem_inc(s_h, 2)
            dve.wait_ge(W.s_const, W.const_count)
            if fp4:
                dve.sem_inc(s_vald, 1)
            else:
                dve.sem_inc(s_lod, 1)

            def decode_gu(i):
                if fp4:
                    dve.wait_ge(s_rawg, 16 * W.loads * (i + 1))
                    W.value(dve, link, raw_gu, "gu", i, s_valg)

            def lo_gu(i, e):
                dve.wait_ge(s_hig, i + 1)
                dve.tensor_tensor(w[e][1][:], val_gu[:], w[e][0][:].bitcast(F32), ALU.subtract).then_inc(s_log, 1)
                if fp4:
                    dve.wait_ge(s_log, i + 1)

            def prep_down(i):
                if fp4:
                    dve.wait_ge(s_rawd, 16 * W.loads * (i + 1))
                    W.value(dve, link, raw_down, "down", i, s_vald)
                dve.wait_ge(s_hid, i + 1)
                at = bass.ds(i, 1)
                dve.tensor_tensor(wd[1][:, at, :].rearrange("p a o -> p (a o)"), val_down[:],
                                  wd[0][:, at, :].bitcast(F32).rearrange("p a o -> p (a o)"), ALU.subtract).then_inc(s_lod, 1)

            def product(i, e, c):
                dve.wait_ge(s_sil, 2 * i + c + 1)
                dve.wait_ge(s_mm, 4 * i + 2 * c + 3)
                dst = hT[:, bass.ds(i, 1), c * 512:(c + 1) * 512].rearrange("p a n -> p (a n)")
                dve.scalar_tensor_tensor(out=dst, in0=gu_ps[c][1][:], scalar=1.0 if fp4 else sc[e][:, 1:2], in1=sil[c][:],
                                         op0=ALU.mult, op1=ALU.mult).then_inc(s_h, 1)

            def scales(i, e):
                if not fp4:
                    if not (isinstance(i, int) and i == 0):
                        dve.wait_ge(s_h, 2 * i)
                    copy_scaled(dve, sc[e][:], W.scales[:, :, bass.ds(i, 1)].rearrange("p a o -> p (a o)")).then_inc(s_sc, 1)
                    dve.wait_ge(s_sc, i + 1)

            def step(i, e, more):
                link.body((2 * i + 1) * W.links)
                if more:
                    decode_gu(i + 1)
                product(i, e, 0)
                if more:
                    lo_gu(i + 1, 1 - e)
                    scales(i + 1, 1 - e)
                prep_down(i)
                product(i, e, 1)
                if fp4 and more:
                    dve.wait_ge(s_lod, i + 1)
            scales(0, 0)
            decode_gu(0)
            lo_gu(0, 0)
            steps(step)(dve)


def layer1_qkv(nc, st, K, src):
    w = [st.sb(f"wqkv{i}", [P, KD, C1], F32R) for i in range(2)]
    split_weights(nc, st, w, src.rearrange("(k p) c -> p k c", p=P), KD, C1, per=1)
    xT, qkv = K["xT"], K["qkv"]
    ps = [[st.ps(f"q{i}"), st.ps(f"kv{i}")] for i in range(2)]
    s_mm, s_q, s_kv = st.sem("mm"), st.sem("q"), st.sem("kv")
    parts = ((0, D), (D, C1))
    with nc.Block() as block:
        @block.tensor
        def _(pe):
            for t in range(NT):
                for a, (lo, up) in enumerate(parts):
                    if t >= 2:
                        pe.wait_ge((s_q, s_kv)[a], t - 1)
                    for k in range(KD):
                        for x, y in PAIRS:
                            mm = pe.matmul(ps[t % 2][a][:, 0:up - lo], xT[x][:, k, t * P:(t + 1) * P], w[y][:, k, lo:up],
                                           start=(k == 0 and (x, y) == PAIRS[0]), stop=(k == KD - 1 and (x, y) == PAIRS[-1]))
                    mm.then_inc(s_mm, 1)

        @block.scalar
        def _(act):
            for t in range(NT):
                act.wait_ge(s_mm, 2 * t + 1)
                act.activation(qkv[:, t, 0:D], ps[t % 2][0][:], ACT.Copy).then_inc(s_q, 1)

        @block.vector
        def _(dve):
            for t in range(NT):
                dve.wait_ge(s_mm, 2 * t + 2)
                dve.tensor_copy(qkv[:, t, D:C1], ps[t % 2][1][:, 0:C1 - D]).then_inc(s_kv, 1)


def layer1_heads(nc, st, K):
    ident, ident_r, ident_b, mask_q, mask_k = (K[x] for x in ("ident", "ident_r", "ident_b", "mask_q", "mask_k"))
    qkv, ctx = K["qkv"], K["ctx"]
    HALF = NT // 2
    MROW = 4 * HD1
    qa = st.sb("qa", [P, NT, GS1, P], F32R)
    ka = st.sb("ka", [P, NT, P], F32R)
    va = [st.sb(f"va{e}", [P, NT, 32]) for e in range(2)]
    qt = [[st.sb(f"qt{e}{j}", [P, N], F32R) for j in range(GS1)] for e in range(2)]
    kt0 = st.sb("kt0", [P, N], F32R)
    ktm = [st.sb(f"ktm{e}", [P, N], F32R) for e in range(2)]
    ex = [[st.sb(f"ex{c}{j}", [P, 512]) for j in range(GS1)] for c in range(2)]
    mx = [st.sb(f"mx{e}", [P, NT, 2]) for e in range(2)]
    mm_ = st.sb("m", [P, NT])
    sums = st.sb("sums", [P, N])
    rden = st.sb("rden", [P, HALF, GS1])
    fill_ps = [st.ps(f"fill{i}") for i in range(2)]
    p1_ps = [st.ps(f"p1{i}") for i in range(2)]
    p2_ps = [st.ps(f"p2{i}") for i in range(2)]
    sum_ps = st.ps("sum", (P, N))

    s_ka, s_qa, s_va, s_m = st.sem("ka"), st.sem("qa"), st.sem("va"), st.sem("mset")
    s_fill, s_free, s_freeo = st.sem("fill"), st.sem("free"), st.sem("freeo")
    s_p1, s_max, s_mq = st.sem("p1"), st.sem("max"), st.sem("mq")
    s_p2, s_exp, s_av, s_sum = st.sem("p2"), st.sem("exp"), st.sem("av"), st.sem("sum")
    s_dve, s_init = st.sem("dve"), st.sem("init")

    P1 = []
    for i in range(NT):
        for lo in range(0, (i + 1) * P, 512):
            used = min(512, (i + 1) * P - lo)
            P1.append((i, lo, max(used, 256), used))
    P2 = []
    for h in range(2):
        for k in range(4 * h + 4):
            first = max(0, k * P - h * 512)
            P2.append((h, k, min(first, 256), first))
    SLOTS, NP1 = len(P2), len(P1)
    p1_slot = [1 + c * (SLOTS - 2) // (GS1 * NP1) for c in range(GS1 * NP1)]
    FILLS = []
    FILLS += [(0, "k", 0)]
    for j in range(GS1):
        FILLS.append((p1_slot[NP1 * j] - 1, "q", j))
        FILLS.append((p1_slot[NP1 * j + NP1 - 1] + 1, "m", j))
    FILLS.append((3, "o", 0))
    FILLS.sort(key=lambda f: f[0])

    def fills(before, after):
        return [f for f in FILLS if (before if f[1] == "o" else after)]

    PREP_FILLS = 2 * (1 + 2 * GS1)

    def base_of(g, before):
        return PREP_FILLS * (g + 1), 2 * (g - 1) if before else 0

    def run_turns(eng, turn):
        turn(0, 0, False, True)
        with eng.Fori(0, (G1 - 2) // 2) as i:
            turn(2 * i + 1, 1, True, True)
            turn(2 * i + 2, 0, True, True)
        turn(G1 - 1, 1, True, False)

    class Banks:

        def __init__(self, g, before, after):
            self.a, self.o = base_of(g, before)
            self.na = self.no = 0

    with nc.Block() as block:
        @block.tensor
        def _(pe):
            pe.sem_inc(s_av, 2)

            def fill(pos, seq, kind, head, e_next, prev_kind, osrc=None):
                a, o = pos
                for h in range(2):
                    if prev_kind == "o":
                        pe.wait_ge(s_freeo, o - 1 + h)
                    elif prev_kind is not None:
                        pe.wait_ge(s_free, a - 1 + h)
                    for t in range(HALF):
                        tile = h * HALF + t
                        if kind == "k":
                            out, src, idn = fill_ps[h][:, t * P:(t + 1) * P].bitcast(F32R), ka[:, tile, :], ident_r
                        elif kind == "o":
                            out, src, idn = fill_ps[h][:, t * P:(t + 1) * P], sums[:, tile * P:(tile + 1) * P], ident
                        else:
                            out, src, idn = fill_ps[h][:, t * P:(t + 1) * P].bitcast(F32R), qa[:, tile, head, :], ident_r
                        tr = pe.transpose(out, src, idn[:])
                    tr.then_inc(s_fill, 1)

            def do_fill(g, f, state):
                _, kind, j = f
                if kind == "k":
                    pe.wait_ge(s_ka, g + 2)
                if kind == "q":
                    pe.wait_ge(s_qa, g + 2)
                if kind == "m":
                    pe.wait_ge(s_mq, GS1 * (g + 1) + j + 1)
                if kind == "o":
                    pe.wait_ge(s_sum, g + 1)
                fill((state[0], state[1]), None, kind, j, None, state[2])
                state[1 if kind == "o" else 0] += 2
                state[2] = kind

            def pass1(g, e, c):
                j, (i, lo, n, used) = c // NP1, P1[c % NP1]
                at = GS1 * NP1 * g + c
                if c % NP1 == 0:
                    pe.wait_ge(s_free, PREP_FILLS * g + FREE_AFTER["q", j])
                pe.wait_ge(s_max, at + 1)
                out = p1_ps[c % 2][:, 0:n]
                diag = i * P - lo
                masked = 0 <= diag < used
                mm = pe.matmul(out, qt[e][j][:, i * P:(i + 1) * P], kt0[:, lo:lo + n], start=True, stop=True)
                if masked:
                    mm = pe.matmul(p1_ps[c % 2][:, diag:diag + P], ident_b[:], mask_q[:], start=False, stop=True, skip_group_check=True)
                mm.then_inc(s_p1, 1)

            def pass2(g, e, s, j):
                h, k, lo, first = P2[s]
                at = GS1 * (SLOTS * g + s) + j
                pe.wait_ge(s_exp, at + 1)
                out = p2_ps[j % 2][:, lo:512]
                diag = k * P - h * 512
                mm = pe.matmul(out, ktm[e][:, k * P:(k + 1) * P], qt[e][j][:, h * 512 + lo:(h + 1) * 512], start=True, stop=True)
                if diag >= 0:
                    mm = pe.matmul(p2_ps[j % 2][:, diag:diag + P], ident_b[:], mask_k[:], start=False, stop=True, skip_group_check=True)
                mm.then_inc(s_p2, 1)

            def weigh(g, e, s):
                h, k, lo, first = P2[s]
                if s == 0:
                    pe.wait_ge(s_sum, g + 1)
                    pe.wait_ge(s_va, g + 1)
                pe.wait_ge(s_exp, GS1 * (SLOTS * g + s) + GS1 + 2)
                for j in range(GS1):
                    mm = pe.matmul(sum_ps[32 * j:32 * j + 32, h * 512 + first:(h + 1) * 512], va[e][:, k, :],
                                   ex[s % 2][j][:, first:512], start=(k == 0), stop=(k == 4 * h + 3))
                mm.then_inc(s_av, 1)

            FREE_AFTER, seen = {}, 0
            for f in fills(False, True):
                seen += 2
                FREE_AFTER[f[1], f[2]] = seen

            def turn(g, e, before, after):
                state = [*base_of(g, before), "o" if (before and not after) else None]
                todo = fills(before, after)
                state[2] = "m"
                nxt = 0
                for s in range(SLOTS):
                    for f in [f for f in todo if f[0] == s]:
                        do_fill(g, f, state)
                    mine = [c for c in range(GS1 * NP1) if after and p1_slot[c] == s]
                    for j in range(GS1):
                        pass2(g, e, s, j)
                        for c in mine[len(mine) * j // GS1:len(mine) * (j + 1) // GS1]:
                            pass1(g + 1, 1 - e, c)
                    if s >= 1:
                        weigh(g, e, s - 1)
                weigh(g, e, SLOTS - 1)

            state = [0, 0, None]
            for f in fills(False, True):
                if f[1] != "m":
                    do_fill(-1, f, state)
                else:
                    do_fill(-1, f, state)
                if f[1] == "q":
                    for c in range(NP1 * f[2], NP1 * (f[2] + 1)):
                        pass1(0, 0, c)
            run_turns(pe, turn)
            pe.wait_ge(s_sum, G1 + 1)
            o = 2 * (G1 - 1)
            fill((PREP_FILLS * G1, o), None, "o", 0, None, "o")

        @block.scalar
        def _(act):
            act.sem_inc(s_exp, 2)
            act.sem_inc(s_sum, 1)

            def read_fill(n, e, kind, j):
                for h in range(2):
                    act.wait_ge(s_fill, n + h + 1)
                    cols = slice(h * 512, (h + 1) * 512)
                    if kind == "k":
                        act.activation(ktm[e][:, cols], fill_ps[h][:], ACT.Copy)
                        act.activation(kt0[0:MROW, cols], fill_ps[h][0:MROW, :], ACT.Copy).then_inc(s_free, 1)
                    elif kind == "q":
                        act.activation(qt[e][j][0:MROW, cols], fill_ps[h][0:MROW, :], ACT.Copy).then_inc(s_free, 1)
                    else:
                        act.activation(qt[e][j][MROW:MROW + 32, cols], fill_ps[h][MROW:MROW + 32, :], ACT.Copy).then_inc(s_free, 1)

            def exps(g, s, j):
                h, k, lo, first = P2[s]
                at = GS1 * (SLOTS * g + s) + j
                act.wait_ge(s_p2, at + 1)
                act.wait_ge(s_av, SLOTS * g + s + 1)
                act.activation(ex[s % 2][j][:, first:512], p2_ps[j % 2][:, first:512], ACT.Exp, scale=HD1 ** -0.5).then_inc(s_exp, 1)

            def turn(g, e, before, after):
                a, o = base_of(g, before)
                n = a + o
                if before:
                    sums_out(g - 1)
                todo = fills(before, after)
                for s in range(SLOTS):
                    for f in [f for f in todo if f[0] == s]:
                        if f[1] != "o":
                            read_fill(n, 1 - e, f[1], f[2])
                        n = n + 2
                    for j in range(GS1):
                        exps(g, s, j)

            def sums_out(g):
                act.wait_ge(s_av, SLOTS * g + SLOTS + 2)
                act.activation(sums[:], sum_ps[:], ACT.Copy).then_inc(s_sum, 1)

            act.wait_ge(s_init, 1)
            n = 0
            for f in fills(False, True):
                read_fill(n, 0, f[1], f[2])
                n += 2
            run_turns(act, turn)
            sums_out(G1 - 1)

        @block.vector
        def _(dve):
            link = Chain(dve, s_dve)
            dve.sem_inc(s_max, 2)
            z = [qa[:].rearrange("p t g c -> p (t g c)"), ka[:].rearrange("p t c -> p (t c)"), kt0[:]]
            z += [q[:] for e in range(2) for q in qt[e]]
            for x in z:
                link(dve.memset(x.bitcast(F32), 0.0))
            link(dve.memset(ka[:, :, MROW:MROW + 2].bitcast(F32), -1.0))
            for e in range(2):
                link(dve.memset(va[e][:], 0.0))
                link(dve.memset(va[e][:, :, HD1:HD1 + 1], 1.0))
                link(dve.memset(mx[e][:], -3.0e38))
            dve.memset(rden[:], 0.0).then_inc(s_init, 1)
            SETUP = link.count

            def build(g, e, n):
                if n is not None:
                    dve.wait_ge(s_fill, n)
                ks = qkv[:, :, bass.ds(D + g * HD1, HD1)]
                vs = qkv[:, :, bass.ds(D + G1 * HD1 + g * HD1, HD1)]
                qs = qkv[:, :, bass.ds(g * GS1 * HD1, GS1 * HD1)].rearrange("p t (j d) -> p t j d", j=GS1)
                part = [slice(i * HD1, (i + 1) * HD1) for i in range(4)]
                link(copy_scaled(dve, ka[:, :, part[0]], ks))
                link(copy_scaled(dve, ka[:, :, part[1]], ks))
                link(dve.tensor_tensor(ka[:, :, part[2]], ks, ka[:, :, part[0]].bitcast(F32), ALU.subtract))
                dve.tensor_tensor(ka[:, :, part[3]], ks, ka[:, :, part[0]].bitcast(F32), ALU.subtract).then_inc(s_ka, 1)
                link(copy_scaled(dve, qa[:, :, :, part[0]], qs))
                link(copy_scaled(dve, qa[:, :, :, part[2]], qs))
                link(dve.tensor_tensor(qa[:, :, :, part[1]], qs, qa[:, :, :, part[0]].bitcast(F32), ALU.subtract))
                dve.tensor_tensor(qa[:, :, :, part[3]], qs, qa[:, :, :, part[0]].bitcast(F32), ALU.subtract).then_inc(s_qa, 1)
                if n is not None:
                    dve.wait_ge(s_av, SLOTS * (g - 1) + 2)
                copy_scaled(dve, va[e][:, :, 0:HD1], vs).then_inc(s_va, 1)
            LINKS_BUILD = 6

            def maxima(g, c):
                j, (i, lo, n, used) = c // NP1, P1[c % NP1]
                at = GS1 * NP1 * g + c
                dve.wait_ge(s_p1, at + 1)
                dve.tensor_reduce(mx[j % 2][:, i, lo // 512:lo // 512 + 1], p1_ps[c % 2][:, 0:used], AX.X, ALU.max).then_inc(s_max, 1)
                if c % NP1 == NP1 - 1:
                    dve.wait_ge(s_max, at + 3)
                    link(dve.tensor_tensor(mm_[:], mx[j % 2][:, :, 0], mx[j % 2][:, :, 1], ALU.max))
                    link(dve.tensor_copy(qa[:, :, j, MROW], mm_[:]))
                    dve.tensor_tensor(qa[:, :, j, MROW + 1], mm_[:], qa[:, :, j, MROW].bitcast(F32), ALU.subtract).then_inc(s_mq, 1)
                    dve.wait_ge(s_mq, GS1 * g + j + 1)
            LINKS_MAX = 2 * GS1

            def output(g, n):
                for h in range(2):
                    dve.wait_ge(s_fill, n + h + 1)
                    f = fill_ps[h][:].rearrange("p (t j c) -> p t j c", t=HALF, j=GS1)
                    link(dve.reciprocal(rden[:], f[:, :, :, HD1]))
                    dst = ctx[:, h * HALF:(h + 1) * HALF, bass.ds(g * GS1 * HD1, GS1 * HD1)].rearrange("p t (j d) -> p t j d", j=GS1)
                    dve.tensor_tensor(dst, f[:, :, :, 0:HD1], rden[:].unsqueeze(3).to_broadcast([P, HALF, GS1, HD1]), ALU.mult).then_inc(s_freeo, 1)
                    dve.wait_ge(s_freeo, 2 * g + h + 1)
            LINKS_OUT = 2

            def turn(g, e, before, after):
                a, o = base_of(g, before)
                n = a + o
                link.body(SETUP + (LINKS_BUILD + LINKS_MAX) * (g + 1) + (LINKS_OUT * (g - 1) if before else 0))
                if after:
                    build(g + 1, 1 - e, n)
                todo = fills(before, after)
                for s in range(SLOTS):
                    for f in [f for f in todo if f[0] == s]:
                        if f[1] == "o":
                            output(g - 1, n)
                        n = n + 2
                    for c in range(GS1 * NP1):
                        if after and p1_slot[c] == s:
                            maxima(g + 1, c)

            build(0, 0, None)
            for c in range(GS1 * NP1):
                maxima(0, c)
            run_turns(dve, turn)
            link.body(SETUP + (LINKS_BUILD + LINKS_MAX) * G1 + LINKS_OUT * (G1 - 1))
            output(G1 - 1, PREP_FILLS * G1 + 2 * (G1 - 1))


def transpose_ctx(nc, st, K):
    ctx, cT, ident = K["ctx"], K["cT"], K["ident"]
    ps = [st.ps(f"t{i}") for i in range(2)]
    s_tr, s_rd = st.sem("ctx_tr"), st.sem("ctx_rd")
    with nc.Block() as block:
        @block.tensor
        def _(pe):
            for t in range(NT):
                if t >= 2:
                    pe.wait_ge(s_rd, t - 1)
                for k in range(KD):
                    tr = pe.transpose(ps[t % 2][:, k * P:(k + 1) * P], ctx[:, t, k * P:(k + 1) * P], ident[:])
                tr.then_inc(s_tr, 1)

        @block.scalar
        def _(act):
            for t in range(NT):
                act.wait_ge(s_tr, t + 1)
                act.activation(cT[:, :, t * P:(t + 1) * P], ps[t % 2][:].rearrange("p (k n) -> p k n", k=KD), ACT.Copy).then_inc(s_rd, 1)


def program(nc, T, out, stages=99):
    ctx = ExitStack()
    with ctx:
        def sb(name, shape, dt=F32):
            return ctx.enter_context(nc.sbuf_tensor(name, shape, dt))

        K = {"ident": sb("ident", [P, P]), "ident_r": sb("ident_r", [P, P], F32R), "ident_b": sb("ident_b", [P, P], BF16),
             "mask_q": sb("mask_q", [P, P], BF16), "mask_k": sb("mask_k", [P, P], BF16), "scal": sb("scal", [P, 3, H0]),
             "ls_iaw": T["ls_iaw"], "ls_hws": T["ls_hws"],
             "xT": [sb("xT_hi", [P, KD, N], F32R), sb("xT_lo", [P, KD, N], F32R)]}
        with Stage(nc, "const") as st:
            constants(nc, st, K)
        mid = [nc.dram_tensor(f"mid{i}", (B, N, D), F32, kind="Internal").ap().rearrange("b (t p) d -> b t p d", p=P) for i in range(3)]
        x0, x4 = (x.rearrange("b (t p) d -> b t p d", p=P) for x in (T["tokens"], out))
        with nc.Fori(0, B) as b:
            def held(c, name, shape, dt=F32):
                K[name] = c.enter_context(nc.sbuf_tensor(f"{name}_{layer}", shape, dt))

            def tile_of(x):
                return lambda t: x[b, t]

            layer = 0
            with Stage(nc, "in") as st:
                finish_tokens(nc, st, K, tile_of(x0), None)
            with ExitStack() as c:
                held(c, "oT", [P, H0, N])
                with Stage(nc, "heads0") as st:
                    layer0_heads(nc, st, K, T["Wqg"], T["Wkv"])
                with Stage(nc, "out0") as st:
                    layer0_out(nc, st, K, tile_of(x0), tile_of(mid[0]), T["Wo0"])
            for layer in range(2):
                if layer == 1:
                    with ExitStack() as c:
                        held(c, "ctx", [P, NT, D])
                        held(c, "qkv", [P, NT, C1])
                        with Stage(nc, "qkv1") as st:
                            layer1_qkv(nc, st, K, T["Wqkv1"])
                        with Stage(nc, "heads1") as st:
                            layer1_heads(nc, st, K)
                        held(c, "cT", [P, KD, N])
                        with Stage(nc, "out1") as st:
                            transpose_ctx(nc, st, K)
                            w = [st.sb(f"wo{i}", [P, KD, D], F32R) for i in range(2)]
                            split_weights(nc, st, w, T["Wo1"].rearrange("(k p) c -> p k c", p=P), KD, D, per=1)
                            finish_tokens(nc, st, K, tile_of(mid[1]), tile_of(mid[2]), kc=KD, src=K["cT"], w=w)
                with ExitStack() as c:
                    held(c, "hT", [P, KI, N])
                    K["wd"] = [c.enter_context(nc.sbuf_tensor(f"wd{i}_{layer}", [P, KI, D], F32R)) for i in range(2)]
                    with Stage(nc, f"gu{layer}") as st:
                        if layer == 0:
                            W = Fp4Weights(nc, st, T["gu_words"], T["gu_scales"], T["down_words"], T["down_scales"], T["shift"])
                        else:
                            W = PlainWeights(nc, st, T["gate1"], T["up1"], T["down1"], T["gate_s"], T["up_s"])
                        gate_up(nc, st, K, W)
                    with Stage(nc, f"down{layer}") as st:
                        if layer == 0:
                            finish_tokens(nc, st, K, tile_of(mid[0]), tile_of(mid[1]), kc=KI, src=K["hT"], w=K["wd"], norm="rms")
                        else:
                            ds = st.sb("down_s", [P, D])
                            s_ds = st.sem("ds")
                            finish_tokens(nc, st, K, tile_of(mid[2]), tile_of(x4), kc=KI, src=K["hT"], w=K["wd"],
                                          y_scale=(ds, T["down_s"], s_ds), more=False)


_IN = ["tokens", "Wqg", "Wkv", "Wo0", "ls_iaw", "ls_hws", "gu_words", "gu_scales", "down_words", "down_scales", "shift",
       "Wqkv1", "Wo1", "gate1", "up1", "down1", "gate_s", "up_s", "down_s"]


def layout(i):
    import numpy as np

    c = np.ascontiguousarray
    return {
        "tokens": i["L0_attn_tokens"], "Wqg": i["L0_attn_Wqg"], "Wkv": i["L0_attn_Wkv"], "Wo0": i["L0_attn_Wo"],
        "ls_iaw": i["L0_attn_ls_iaw"], "ls_hws": i["L0_attn_ls_hws"],
        "gu_words": c(i["L0_ffn_gate_up_packed"].T.reshape(KD, 16, 2, KI, P).transpose(3, 1, 0, 2, 4)).reshape(KI, 16, KD * 2 * P),
        "gu_scales": c(i["L0_ffn_gate_up_scales"].reshape(KD, 2, KI, P).transpose(2, 0, 1, 3)).reshape(KI, KD * 2 * P),
        "down_words": c(i["L0_ffn_down_packed"].T), "down_scales": i["L0_ffn_down_scales"],
        "shift": np.array([[28 - 4 * (p % 8)] for p in range(P)], np.int32),
        "Wqkv1": c(np.concatenate([i["L1_attn_Wq"], i["L1_attn_Wk"], i["L1_attn_Wv"]], axis=0).T),
        "Wo1": c(i["L1_attn_Wo"].T), "gate1": c(i["L1_ffn_gate_w"].T), "up1": c(i["L1_ffn_up_w"].T),
        "down1": c(i["L1_ffn_down_w"].T), "gate_s": c(i["L1_ffn_gate_s"].reshape(KI, P).T), "up_s": c(i["L1_ffn_up_s"].reshape(KI, P).T), "down_s": i["L1_ffn_down_s"],
    }


def kernel(**inputs):
    import numpy as np
    import concourse.bacc as bacc
    from concourse.bass_utils import run_bass_kernel_spmd

    nc = bacc.Bacc("TRN2", target_bir_lowering=False, num_devices=1)
    arrays = layout({k: np.asarray(v) for k, v in inputs.items()})
    T = {k: nc.dram_tensor(f"in_{k}", arrays[k].shape, mybir.dt.from_np(arrays[k].dtype), kind="ExternalInput").ap() for k in _IN}
    out = nc.dram_tensor("out_x", (B, N, D), F32, kind="ExternalOutput").ap()
    program(nc, T, out)
    r = run_bass_kernel_spmd(nc, [{f"in_{k}": arrays[k] for k in _IN}], core_ids=[0])
    return r.results[0]["out_x"]
```

```python
import math
from contextlib import ExitStack

import concourse.bass as bass
from concourse import mybir

F32 = mybir.dt.float32
F32R = mybir.dt.float32r
BF16 = mybir.dt.bfloat16
F16 = mybir.dt.float16
I32 = mybir.dt.int32
ALU = mybir.AluOpType
ACT = mybir.ActivationFunctionType
AX = mybir.AxisListType

P = 128
B, N, D = 2, 1024, 512
NT = N // P
KD = D // P
H0, DK, DV = 16, 64, 128
HW = DK + DV
INTER = 1408
KI = INTER // P
G1, GS1, HD1 = 8, 4, 16
C1 = D + 2 * G1 * HD1
LN_EPS, RMS_EPS, NORM_EPS = 1e-5, 1e-6, 1e-12
RSQRT_MAGIC = float(0x5F3759DF)
PAIRS = ((0, 0), (0, 1), (1, 0))


class Stage:

    def __init__(self, nc, name):
        self.nc, self.name, self.ctx, self.sems = nc, name, ExitStack(), []

    def __enter__(self):
        return self

    def __exit__(self, *e):
        if e[0] is None:
            for s in self.sems:
                self.nc.sync.sem_clear(s)
            self.nc.all_engine_barrier()
        return self.ctx.__exit__(*e)

    def sb(self, name, shape, dt=F32):
        return self.ctx.enter_context(self.nc.sbuf_tensor(f"{self.name}_{name}", shape, dt))

    def ps(self, name, shape=(P, 512), dt=F32):
        return self.ctx.enter_context(self.nc.psum_tensor(f"{self.name}_{name}", list(shape), dt))

    def sem(self, name):
        s = self.ctx.enter_context(self.nc.semaphore(f"{self.name}_{name}"))
        self.sems.append(s)
        return s


class Chain:

    def __init__(self, eng, sem):
        self.eng, self.sem, self.count, self.base = eng, sem, 0, 0

    def __call__(self, ins):
        self.mark(ins)
        self.settle()

    def mark(self, ins):
        ins.then_inc(self.sem, 1)
        self.count += 1

    def settle(self):
        self.eng.wait_ge(self.sem, self.base + self.count)

    def body(self, base):
        self.base, self.count = base, 0


def rsqrt(link, dve, y, x, tmp):
    link(dve.tensor_scalar(y.bitcast(I32), x.bitcast(I32), -0.5, RSQRT_MAGIC, ALU.mult, ALU.add))
    for _ in range(3):
        link(dve.scalar_tensor_tensor(out=tmp, in0=y, scalar=-0.5, in1=x, op0=ALU.mult, op1=ALU.mult))
        link(dve.tensor_tensor(tmp, tmp, y, ALU.mult))
        link(dve.scalar_tensor_tensor(out=y, in0=tmp, scalar=1.5, in1=y, op0=ALU.add, op1=ALU.mult))


RSQRT_LINKS = 10

_S2 = -(0.5 ** (1 / 3))
_S1 = (-_S2 / 2) ** (1 / 3)
_S0 = -((_S1 / 2) ** (1 / 3))
COLUMN_SCALES = (_S0, _S1, _S2)
COLUMN_MAGIC = RSQRT_MAGIC + math.log2(-_S0) * 2 ** 23 - 2.0 ** 31


def rsqrt_column(link, dve, y, x, tmp):
    link(dve.tensor_scalar(y.bitcast(I32), x.bitcast(I32), -0.5, COLUMN_MAGIC, ALU.mult, ALU.add))
    for scale in COLUMN_SCALES:
        link(dve.scalar_tensor_tensor(out=tmp, in0=x, scalar=y, in1=y, op0=ALU.mult, op1=ALU.mult))
        link(dve.scalar_tensor_tensor(out=y, in0=tmp, scalar=-3 * scale * scale, in1=y, op0=ALU.add, op1=ALU.mult))


COLUMN_LINKS = 7


def copy_scaled(dve, out, in_):
    return dve.tensor_scalar(out, in_, 1.0, None, ALU.mult)


def constants(nc, st, K):
    s_fill, s_ident, s_scal, s_e, s_fillm = (st.sem(n) for n in ("fill", "ident", "scal", "e", "fillm"))
    raw = st.sb("raw", [P, 2, H0])
    with nc.Block() as block:
        @block.sync
        def _(sp):
            for j, name in enumerate(("ls_iaw", "ls_hws")):
                sp.dma_start(raw[:, j, :], K[name].rearrange("(o h) -> o h", o=1).to_broadcast([P, H0])).then_inc(s_scal, 16)

        @block.gpsimd
        def _(pool):
            pool.memset(K["ident"][:], 0.0).then_inc(s_fill, 1)
            pool.wait_ge(s_fill, 1)
            pool.affine_select(out=K["ident"][:], in_=K["ident"][:], compare_op=ALU.not_equal, fill=1.0,
                               base=0, pattern=[[-1, P]], channel_multiplier=1).then_inc(s_ident, 1)
            for name, sign in (("mask_q", 1), ("mask_k", -1)):
                m = K[name]
                pool.memset(m[:], 0.0).then_inc(s_fillm, 1)
                pool.wait_ge(s_fillm, 1 if sign == 1 else 3)
                pool.affine_select(out=m[:], in_=m[:], compare_op=ALU.is_ge, fill=-1.0e30, base=0,
                                   pattern=[[-sign, P]], channel_multiplier=sign).then_inc(s_fillm, 1)

        @block.scalar
        def _(act):
            act.wait_ge(s_scal, 32)
            act.activation(K["scal"][:, 0:2, :], raw[:], ACT.Exp).then_inc(s_e, 1)

        @block.vector
        def _(dve):
            dve.wait_ge(s_ident, 1)
            dve.tensor_copy(K["ident_r"][:], K["ident"][:])
            dve.tensor_copy(K["ident_b"][:], K["ident"][:])
            dve.wait_ge(s_e, 1)
            link = Chain(dve, s_fill)
            link.body(1)
            link(dve.tensor_scalar(K["scal"][:, 2, :], K["scal"][:, 0, :], 1.0, None, ALU.add))
            link(dve.reciprocal(K["scal"][:, 0, :], K["scal"][:, 2, :]))
            link(dve.tensor_scalar(K["scal"][:, 2, :], K["scal"][:, 0, :], -1.0, 1.0, ALU.mult, ALU.add))


def finish_tokens(nc, st, K, x_in, x_out, *, kc=0, src=None, w=None, norm="layer", y_scale=None, more=True,
                  weights=None, transpose=None):
    ident, xT = K["ident"], K["xT"]
    product = kc > 0
    chunks = ((0, (kc + 1) // 2), ((kc + 1) // 2, kc))
    if product:
        lhs = [[st.sb(f"lhs{c}{part}", [P, chunks[c][1] - chunks[c][0], P], F32R) for part in range(2)] for c in range(2)]
        y_ps = [st.ps(f"y{i}") for i in range(2)]
    x_sb = [st.sb(f"x{i}", [P, D]) for i in range(2)]
    new_sb = [st.sb(f"new{i}", [P, D]) for i in range(2)]
    hat_sb = [st.sb(f"hat{i}", [P, D]) for i in range(2)]
    u_sb = [st.sb(f"u{i}", [P, D]) for i in range(2)] if product else x_sb
    y_sb = st.sb("ysb", [P, D]) if y_scale is not None else None
    tr_ps = [st.ps(f"tr{i}") for i in range(2)]
    spare = st.sb("spare", [P, 1])
    stats, mv = st.sb("stats", [P, 2, 6]), st.sb("mv", [P, 2, 2])
    sm = [st.sb(f"sm{i}", [P, 4, 2]) for i in range(2)]
    s_load, s_store = [st.sem("load0"), st.sem("load1")], [st.sem("store0"), st.sem("store1")]
    s_u, s_new, s_stat, s_hat, s_tr = st.sem("u"), st.sem("new"), st.sem("stat"), st.sem("hat"), st.sem("tr")
    s_lhs_hi, s_lhs_lo, s_mm = st.sem("lhs_hi"), st.sem("lhs_lo"), st.sem("mm")
    s_xt_hi, s_xt_lo, s_dve = st.sem("xt_hi"), st.sem("xt_lo"), st.sem("dve")

    def tiles(eng, body):
        body(0, 0, 0)
        body(1, 1, 0)
        with eng.Fori(1, NT // 2 - 1) as i:
            body(2 * i, 0, i)
            body(2 * i + 1, 1, i)
        body(NT - 2, 0, NT // 2 - 1)
        body(NT - 1, 1, NT // 2 - 1)

    def last(t):
        return isinstance(t, int) and t == NT - 1

    def first(t):
        return isinstance(t, int) and t == 0

    with nc.Block() as block:
        @block.sync
        def _(sp):
            sp.sem_inc(s_store[0], 16)
            sp.sem_inc(s_store[1], 16)
            if weights:
                weights.load(sp)
            sp.dma_start(x_sb[0][:], x_in(0)).then_inc(s_load[0], 16)
            if y_scale is not None:
                sp.dma_start(y_scale[0][:], y_scale[1].unsqueeze(0).to_broadcast([P, D])).then_inc(y_scale[2], 16)

            def body(t, p, h):
                if not last(t):
                    if not first(t):
                        sp.wait_ge(*((s_u, t + 1) if product else (s_hat, t + 2)))
                    sp.dma_start(x_sb[1 - p][:], x_in(t + 1)).then_inc(s_load[1 - p], 16)
                if x_out is not None:
                    sp.wait_ge(s_new, t + 3)
                    sp.dma_start(x_out(t), new_sb[p][:]).then_inc(s_store[p], 16)
            tiles(sp, body)
            if x_out is not None:
                for p in range(2):
                    sp.wait_ge(s_store[p], 16 + 16 * (NT // 2))

        @block.tensor
        def _(pe):
            def products(t, p):
                for c, (a, b) in enumerate(chunks):
                    pe.wait_ge(s_lhs_lo, 2 * t + c + 1)
                    if c == 0 and not first(t):
                        pe.wait_ge(s_u, t)
                    for k in range(a, b):
                        if weights and first(t):
                            weights.ready(pe, k)
                        for i, j in PAIRS:
                            mm = pe.matmul(y_ps[p][:], lhs[c][i][:, k - a, :], w[j][:, k, :],
                                           start=(k == 0 and (i, j) == PAIRS[0]), stop=(k == kc - 1 and (i, j) == PAIRS[-1]))
                    mm.then_inc(s_mm, 1)

            def transposes(t, p):
                pe.wait_ge(s_hat, t + 3)
                pe.wait_ge(s_xt_lo, t + 1)
                for k in range(KD):
                    tr = pe.transpose(tr_ps[p][:, k * P:(k + 1) * P], hat_sb[p][:, k * P:(k + 1) * P], ident[:])
                tr.then_inc(s_tr, 1)

            def body(t, p, h):
                if product:
                    products(t, p)
                if more and product and not (first(t) or first(t - 1)):
                    transposes(t - 2, p)
                if more and not product and not first(t):
                    transposes(t - 1, 1 - p)
            if transpose:
                transpose.transposes(pe)
            tiles(pe, body)
            if more and product:
                transposes(NT - 2, 0)
            if more:
                transposes(NT - 1, 1)

        @block.scalar
        def _(act):
            def split_hi(t):
                for c, (a, b) in enumerate(chunks):
                    act.wait_ge(s_mm, 2 * t + c + 1)
                    act.activation(lhs[c][0][:], src[:, a:b, bass.ds(t * P, P)], ACT.Copy).then_inc(s_lhs_hi, 1)

            def xt_hi(t, p):
                act.wait_ge(s_tr, t + 1)
                act.activation(xT[0][:, :, bass.ds(t * P, P)], tr_ps[p][:].rearrange("p (k n) -> p k n", k=KD),
                               ACT.Copy).then_inc(s_xt_hi, 1)

            def body(t, p, h):
                if product and not last(t):
                    split_hi(t + 1)
                if product:
                    if more and not (first(t) or first(t - 1)):
                        xt_hi(t - 2, p)
                    if more and not first(t):
                        hat(t - 1, 1 - p, p)
                    act.wait_ge(s_u, t + 2)
                    act.wait_ge(s_store[p], 16 * h + 16)
                    act.activation(new_sb[p][:], u_sb[p][:], ACT.Identity, bias=sm[p][:, 1, 0:1]).then_inc(s_new, 1)
                else:
                    if not first(t):
                        xt_hi(t - 1, 1 - p)
                    hat(t, p, p)

            def hat(t, p, e):
                act.wait_ge(s_stat, t + 1)
                act.activation(hat_sb[p][:], u_sb[p][:], ACT.Identity, bias=sm[e][:, 1, 1:2], scale=sm[e][:, 0, 1:2]).then_inc(s_hat, 1)

            act.sem_inc(s_new, 2)
            act.sem_inc(s_hat, 2)
            if product:
                act.sem_inc(s_mm, 2)
                if transpose:
                    transpose.copies(act)
                split_hi(0)
                if weights:
                    weights.split_hi(act)
            tiles(act, body)
            if product and more:
                xt_hi(NT - 2, 0)
                hat(NT - 1, 1, 0)
            if more:
                xt_hi(NT - 1, 1)

        @block.vector
        def _(dve):
            link = Chain(dve, s_dve)

            def split_lo(t):
                for c, (a, b) in enumerate(chunks):
                    dve.wait_ge(s_lhs_hi, 2 * t + c + 1)
                    dve.tensor_tensor(lhs[c][1][:], src[:, a:b, bass.ds(t * P, P)], lhs[c][0][:].bitcast(F32),
                                      ALU.subtract).then_inc(s_lhs_lo, 1)

            def xt_lo(t, p):
                dve.wait_ge(s_xt_hi, t + 1)
                dst = bass.ds(t * P, P)
                dve.tensor_tensor(xT[1][:, :, dst], tr_ps[p][:].rearrange("p (k n) -> p k n", k=KD),
                                  xT[0][:, :, dst].bitcast(F32), ALU.subtract).then_inc(s_xt_lo, 1)

            def moments(sources):
                for i, x in sources:
                    link.mark(dve.bn_stats(stats[:, i, :], x))
                link.settle()
                dve.memset(spare[:], 0.0)
                for i, x in sources:
                    link.mark(dve.bn_aggr(mv[:, i, :], stats[:, i, :]))
                link.settle()

            def u_stats(t, e):
                moments([(1, u_sb[1 if last(t) else 0 if first(t) else e][:])])
                var = sm[e][:, 2, 1:2]
                link(dve.tensor_scalar(var, mv[:, 1, 1:2], LN_EPS, None, ALU.add))
                rsqrt_column(link, dve, sm[e][:, 0, 1:2], var, sm[e][:, 3, 1:2])
                shifts(e, 1, 2).then_inc(s_stat, 1)

            def shifts(e, lo, up):
                return dve.scalar_tensor_tensor(out=sm[e][:, 1, lo:up], in0=mv[:, lo:up, 0], scalar=-1.0, in1=sm[e][:, 0, lo:up],
                                                op0=ALU.mult, op1=ALU.mult)

            def body(t, p, h):
                if product and not last(t):
                    split_lo(t + 1)
                dve.wait_ge(s_load[p], 16 * h + 16)
                dve.wait_ge(s_hat if more else s_new, t + 1)
                link.body(BODY * t - (0 if first(t) else SKIPPED))
                if not product:
                    u_stats(t, p)
                    if not first(t):
                        xt_lo(t - 1, 1 - p)
                    return
                both = more and not first(t)
                n = 2 if both else 1
                rstd, var, tmp = (sm[p][:, c, 0:n] for c in (0, 2, 3))
                dve.wait_ge(s_mm, 2 * t + 4)
                y = y_ps[p][:]
                if y_scale is not None:
                    link(dve.tensor_tensor(y_sb[:], y, y_scale[0][:], ALU.mult))
                    y = y_sb[:]
                moments([(0, y)] + ([(1, u_sb[1 - p][:])] if both else []))
                if norm == "rms":
                    if both:
                        link.mark(dve.tensor_scalar(var[:, 1:2], mv[:, 1, 1:2], LN_EPS, None, ALU.add))
                    vy, mean_y, var_y = var[:, 0:1], mv[:, 0, 0:1], mv[:, 0, 1:2]
                    link(dve.tensor_scalar(vy, mean_y, mean_y, var_y, ALU.mult, ALU.add))
                    link(dve.tensor_scalar(vy, vy, RMS_EPS, LN_EPS, ALU.add, ALU.mult))
                    link(dve.tensor_tensor(vy, vy, var_y, ALU.add))
                else:
                    link(dve.tensor_scalar(var, mv[:, 0:n, 1], LN_EPS, None, ALU.add))
                if more:
                    rsqrt(link, dve, rstd, var, tmp)
                else:
                    rsqrt_column(link, dve, rstd, var, tmp)
                shift = shifts(p, 0, n)
                if both:
                    shift.then_inc(s_stat, 1)
                dve.scalar_tensor_tensor(out=u_sb[p][:], in0=y, scalar=rstd[:, 0:1], in1=x_sb[p][:], op0=ALU.mult, op1=ALU.add).then_inc(s_u, 1)
                dve.wait_ge(s_u, t + 2)
                assert link.count == BODY - (SKIPPED if first(t) else 0), link.count
                if more and not (first(t) or first(t - 1)):
                    xt_lo(t - 2, p)

            SKIPPED = 2 + (norm == "rms") if product and more else 0
            if product:
                BODY = (y_scale is not None) + 2 + (3 if norm == "rms" else 1) + (RSQRT_LINKS if more else COLUMN_LINKS) + SKIPPED
            else:
                BODY = 2 + 1 + COLUMN_LINKS
            if more:
                dve.sem_inc(s_xt_lo, 2)
            if product:
                dve.sem_inc(s_u, 1)
                split_lo(0)
                if weights:
                    weights.split_lo(dve)
            if y_scale is not None:
                dve.wait_ge(y_scale[2], 16)
            tiles(dve, body)
            if product and more:
                dve.wait_ge(s_hat, NT + 1)
                link.body(BODY * NT - SKIPPED)
                u_stats(NT - 1, 0)
                xt_lo(NT - 2, 0)
            if more:
                xt_lo(NT - 1, 1)


def layer0_heads(nc, st, K, Wqg, Wkv):
    ident, ident_r, xT, scal, oT = K["ident"], K["ident_r"], K["xT"], K["scal"], K["oT"]
    HALF = NT // 2
    SQ, SK, SV, SG = 0, DK, 2 * DK, 2 * DK + DV
    W3 = 2 * HW
    w_raw = st.sb("w_raw", [P, KD, W3])
    w = [st.sb(f"w{i}", [P, KD, W3], F32R) for i in range(2)]
    qkvg = st.sb("qkvg", [P, NT, W3])
    sq = st.sb("sq", [P, HALF, 4, DK])
    ss = st.sb("ss", [P, HALF, 4])
    rn = st.sb("rn", [P, HALF, 4])
    tmp4 = st.sb("tmp4", [P, HALF, 4])
    qkn = st.sb("qkn", [P, HALF, 2, DK])
    qks = st.sb("qks", [P, NT, 2, 3, DK], F32R)
    vn = [st.sb(f"vn{i}", [P, NT, DV]) for i in range(2)]
    gate = [st.sb(f"gate{i}", [P, NT, DV]) for i in range(2)]
    q_hl = [st.sb(f"q_hl{i}", [P, N], F32R) for i in range(2)]
    q_lh = [st.sb(f"q_lh{i}", [P, N], F32R) for i in range(2)]
    k_hl = st.sb("k_hl", [P, N], F32R)
    aff = [st.sb(f"aff{i}", [P, N]) for i in range(2)]
    attn = [st.sb(f"attn{i}", [P, N]) for i in range(2)]
    agg = st.sb("agg", [P, NT, DV])
    osc = st.sb("osc", [P, NT, DV])
    e_ss, e_rn, e_n, e_tn, e_tmp = (st.sb(f"e{i}", [P, NT]) for i in range(5))
    hc = [st.sb(f"hc{i}", [P, 3]) for i in range(2)]
    fill_ps = [st.ps(f"fill{i}") for i in range(2)]
    sim_ps = [st.ps(f"sim{i}", (P, N)) for i in range(2)]
    agg_ps = st.ps("agg_ps", (P, NT, DV))

    s_wraw, s_whi, s_wlo = st.sem("wraw"), st.sem("whi"), st.sem("wlo")
    s_fill, s_free = st.sem("fill"), st.sem("free")
    s_sim, s_aff, s_attn, s_core = st.sem("sim"), st.sem("aff"), st.sem("attn"), st.sem("core")
    s_sq, s_sums, s_qks, s_vn = st.sem("sq"), st.sem("sums"), st.sem("qks"), st.sem("vn")
    s_th, s_silu, s_gate = st.sem("th"), st.sem("silu"), st.sem("gate")
    s_agg, s_asq, s_n, s_tn, s_o = st.sem("agg"), st.sem("asq"), st.sem("n"), st.sem("tn"), st.sem("o")
    s_hc, s_dve = st.sem("hc"), st.sem("dve")

    PREP, OUT = NT + 6, 2

    def fill_base(n, before):
        return (PREP + OUT) * n + PREP - (OUT if before else 0)

    LOOPED = H0 - 4

    def run_turns(eng, turn):
        turn(0, 0, False, True, True)
        with eng.Fori(0, LOOPED // 2) as i:
            turn(2 * i + 1, 1, True, True, True)
            turn(2 * i + 2, 0, True, True, True)
        turn(H0 - 3, 1, True, True, True)
        turn(H0 - 2, 0, True, True, False)
        turn(H0 - 1, 1, True, False, False)

    with nc.Block() as block:
        @block.sync
        def _(sp):
            wq = Wqg.rearrange("(k p) c -> p k c", p=P)
            wk = Wkv.rearrange("(k p) c -> p k c", p=P)

            def load(n):
                sp.dma_start(w_raw[:, :, SQ:SQ + DK], wq[:, :, bass.ds(n * HW, DK)]).then_inc(s_wraw, 16)
                sp.dma_start(w_raw[:, :, SG:SG + DV], wq[:, :, bass.ds(n * HW + DK, DV)]).then_inc(s_wraw, 16)
                sp.dma_start(w_raw[:, :, SK:SK + HW], wk[:, :, bass.ds(n * HW, HW)]).then_inc(s_wraw, 16)
            load(0)
            with sp.Fori(1, H0) as n:
                sp.wait_ge(s_wlo, n)
                load(n)

        @block.tensor
        def _(pe):
            pe.sem_inc(s_core, 2)

            def project(n, j, base):
                if j == 0:
                    pe.wait_ge(s_wlo, n + 1)
                pe.wait_ge(s_free, base + j + 1)
                out = fill_ps[j % 2][:, 0:W3]
                for k in range(KD):
                    for x, y in PAIRS:
                        mm = pe.matmul(out, xT[x][:, k, j * P:(j + 1) * P], w[y][:, k, :],
                                       start=(k == 0 and (x, y) == PAIRS[0]), stop=(k == KD - 1 and (x, y) == PAIRS[-1]))
                mm.then_inc(s_fill, 1)

            def transposes_qk(n, half, base):
                pe.wait_ge(s_qks, 2 * n + half + 1)
                for f in range(3):
                    pe.wait_ge(s_free, base + f + 1)
                    for t in range(HALF):
                        src = qks[:, half * HALF + t, f // 2, f % 2:f % 2 + 2, :]
                        tr = pe.transpose(fill_ps[(half + f) % 2][:, t * P:(t + 1) * P].bitcast(F32R), src, ident_r[:])
                    tr.then_inc(s_fill, 1)

            def transposes_out(n, base):
                pe.wait_ge(s_o, n + 1)
                for f in range(2):
                    pe.wait_ge(s_free, base + f + 1)
                    for t in range(HALF):
                        tr = pe.transpose(fill_ps[f][:, t * P:(t + 1) * P], osc[:, f * HALF + t, :], ident[:])
                    tr.then_inc(s_fill, 1)

            def similar(n, e, j):
                pe.wait_ge(s_aff, NT * n + j + 1)
                for c in range(2):
                    out, cols = sim_ps[j % 2][:, c * 512:(c + 1) * 512], slice(c * 512, (c + 1) * 512)
                    pe.matmul(out, k_hl[:, j * P:(j + 1) * P], q_hl[e][:, cols], start=True, stop=False)
                    mm = pe.matmul(out, k_hl[:, j * P:(j + 1) * P], q_lh[e][:, cols], start=False, stop=True)
                mm.then_inc(s_sim, 1)

            def aggregate(n, e, j):
                if j == 0:
                    pe.wait_ge(s_agg, n + 1)
                    pe.wait_ge(s_vn, n + 1)
                pe.wait_ge(s_attn, NT * n + j + 3)
                for t in range(NT):
                    mm = pe.matmul(agg_ps[:, t, :], attn[j % 2][:, t * P:(t + 1) * P], vn[e][:, j, :],
                                   start=(j == 0 and t % HALF == 0), stop=(j == NT - 1), skip_group_check=True)
                mm.then_inc(s_core, 1)

            def turn(n, e, before, after, more):
                base = fill_base(n, before)
                out_base = base + (NT if after else 0)
                qk_base = base + NT + (OUT if before else 0)
                for j in range(NT):
                    if after and j < 4:
                        project(n + 1, 2 * j, base)
                        project(n + 1, 2 * j + 1, base)
                    if before and j == 4:
                        transposes_out(n - 1, out_base)
                    if after and j == 5:
                        transposes_qk(n + 1, 0, qk_base)
                    if after and j == 7:
                        transposes_qk(n + 1, 1, qk_base + 3)
                    if j < NT - 1:
                        similar(n, e, j + 1)
                    aggregate(n, e, j)
                if after:
                    pe.wait_ge(s_free, qk_base + 6 + 2)
                    similar(n + 1, 1 - e, 0)

            for j in range(NT):
                project(0, j, 0)
            transposes_qk(0, 0, NT)
            transposes_qk(0, 1, NT + 3)
            pe.wait_ge(s_free, PREP + 2)
            similar(0, 0, 0)
            run_turns(pe, turn)
            transposes_out(H0 - 1, fill_base(H0 - 1, True) + OUT)

        @block.scalar
        def _(act):
            act.sem_inc(s_free, 2)
            act.sem_inc(s_aff, 2)
            act.sem_inc(s_agg, 1)

            def weights_hi(n):
                act.wait_ge(s_wraw, 48 * n + 48)
                act.activation(w[0][:], w_raw[:], ACT.Copy).then_inc(s_whi, 1)

            def read_projected(n, j, base):
                if j == 0 and not (isinstance(n, int) and n == 0):
                    act.wait_ge(s_vn, n)
                act.wait_ge(s_fill, base + j + 1)
                act.activation(qkvg[:, j, :], fill_ps[j % 2][:, 0:W3], ACT.Copy).then_inc(s_free, 1)

            def squares(n, half, base):
                act.wait_ge(s_free, base + (half + 1) * HALF + 2)
                act.wait_ge(s_sums, 2 * n + half + 1)
                act.activation(sq[:].rearrange("p t a d -> p t (a d)"), qkvg[:, half * HALF:(half + 1) * HALF, 0:SG],
                               ACT.Square).then_inc(s_sq, 1)

            def read_qk(e, half, base):
                cols = slice(half * 512, (half + 1) * 512)
                for f, dst in enumerate((q_hl[e], q_lh[e], k_hl)):
                    act.wait_ge(s_fill, base + f + 1)
                    act.activation(dst[:, cols], fill_ps[(half + f) % 2][:], ACT.Copy).then_inc(s_free, 1)

            def read_out(n, base):
                for f in range(2):
                    act.wait_ge(s_fill, base + f + 1)
                    act.activation(oT[:, bass.ds(n, 1), f * 512:(f + 1) * 512].rearrange("p a n -> p (a n)"),
                                   fill_ps[f][:], ACT.Copy).then_inc(s_free, 1)

            def affinity(n, e, j):
                act.wait_ge(s_sim, NT * n + j + 1)
                act.wait_ge(s_attn, NT * n + j + 1)
                if j == 0:
                    act.wait_ge(s_hc, n + 1)
                act.activation(aff[j % 2][:], sim_ps[j % 2][:], ACT.Relu, bias=hc[e][:, 2:3]).then_inc(s_aff, 1)

            def gate_tanh(e):
                act.activation(gate[e][:], qkvg[:, :, SG:W3], ACT.Tanh, scale=0.5).then_inc(s_th, 1)

            def gate_final(n, e):
                act.wait_ge(s_silu, n + 1)
                act.activation(gate[e][:], gate[e][:], ACT.Tanh, scale=0.5).then_inc(s_gate, 1)

            def sums_out(n):
                act.wait_ge(s_core, NT * n + NT + 2)
                act.activation(agg[:], agg_ps[:], ACT.Copy).then_inc(s_agg, 1)
                act.wait_ge(s_agg, n + 2)
                act.activation(osc[:], agg[:], ACT.Square).then_inc(s_asq, 1)

            def norm_tanh(n):
                act.wait_ge(s_n, n + 1)
                act.activation(e_tn[:], e_n[:], ACT.Tanh).then_inc(s_tn, 1)

            def turn(n, e, before, after, more):
                base = fill_base(n, before)
                out_base = base + (NT if after else 0)
                qk_base = base + NT + (OUT if before else 0)
                if before:
                    sums_out(n - 1)
                for j in range(NT):
                    if after and j == 2:
                        squares(n + 1, 0, base)
                    if after and j < 4:
                        read_projected(n + 1, 2 * j, base)
                        read_projected(n + 1, 2 * j + 1, base)
                    if before and j == 1:
                        norm_tanh(n - 1)
                    if after and j == 4:
                        squares(n + 1, 1, base)
                    if before and j == 4:
                        read_out(n - 1, out_base)
                    if after and j == 5:
                        read_qk(1 - e, 0, qk_base)
                        gate_tanh(1 - e)
                    if more and j == 6:
                        weights_hi(n + 2)
                    if after and j == 7:
                        read_qk(1 - e, 1, qk_base + 3)
                        gate_final(n + 1, 1 - e)
                    if j < NT - 1:
                        affinity(n, e, j + 1)
                if after:
                    affinity(n + 1, 1 - e, 0)

            weights_hi(0)
            for j in range(NT):
                read_projected(0, j, 0)
                if j == HALF:
                    squares(0, 0, 0)
            squares(0, 1, 0)
            weights_hi(1)
            read_qk(0, 0, NT)
            gate_tanh(0)
            read_qk(0, 1, NT + 3)
            gate_final(0, 0)
            affinity(0, 0, 0)
            run_turns(act, turn)
            sums_out(H0 - 1)
            norm_tanh(H0 - 1)
            read_out(H0 - 1, fill_base(H0 - 1, True) + OUT)

        @block.vector
        def _(dve):
            dve.sem_inc(s_attn, 2)
            dve.sem_inc(s_sums, 1)
            link = Chain(dve, s_dve)

            def weights_lo(n):
                dve.wait_ge(s_whi, n + 1)
                dve.tensor_tensor(w[1][:], w_raw[:], w[0][:].bitcast(F32), ALU.subtract).then_inc(s_wlo, 1)

            def scalars(n, e):
                copy_scaled(dve, hc[e][:], scal[:, :, bass.ds(n, 1)].rearrange("p a o -> p (a o)")).then_inc(s_hc, 1)
                dve.wait_ge(s_hc, n + 1)

            def norms(n, e, half):
                dve.wait_ge(s_sq, 2 * n + half + 1)
                dve.tensor_reduce(ss[:], sq[:], AX.X, ALU.add).then_inc(s_sums, 1)
                dve.wait_ge(s_sums, 2 * n + half + 2)
                link(dve.tensor_tensor(ss[:, :, 2], ss[:, :, 2], ss[:, :, 3], ALU.add))
                rsqrt(link, dve, rn[:], ss[:], tmp4[:])
                link(dve.tensor_scalar(rn[:], rn[:], 1 / NORM_EPS, None, ALU.min))
                link(dve.tensor_scalar(rn[:, :, 0], rn[:, :, 0], hc[e][:, 0:1], None, ALU.mult))

            def split_qk(n, half):
                tiles = slice(half * HALF, (half + 1) * HALF)
                link(dve.tensor_tensor(qkn[:], qkvg[:, tiles, 0:SV].rearrange("p t (a d) -> p t a d", a=2),
                                       rn[:, :, 0:2].unsqueeze(3).to_broadcast([P, HALF, 2, DK]), ALU.mult))
                link(dve.tensor_copy(qks[:, tiles, :, 0, :], qkn[:]))
                link(dve.tensor_tensor(qks[:, tiles, :, 1, :], qkn[:], qks[:, tiles, :, 0, :].bitcast(F32), ALU.subtract))
                dve.tensor_copy(qks[:, tiles, :, 2, :], qkn[:]).then_inc(s_qks, 1)

            def values(n, e, half):
                tiles = slice(half * HALF, (half + 1) * HALF)
                ins = dve.tensor_tensor(vn[e][:, tiles, :], qkvg[:, tiles, SV:SG],
                                        rn[:, :, 2:3].to_broadcast([P, HALF, DV]), ALU.mult)
                if half:
                    ins.then_inc(s_vn, 1)
                    dve.wait_ge(s_vn, n + 1)
                else:
                    link(ins)

            def silu2(n, e):
                dve.wait_ge(s_th, n + 1)
                dve.scalar_tensor_tensor(out=gate[e][:], in0=gate[e][:], scalar=1.0, in1=qkvg[:, :, SG:W3],
                                         op0=ALU.add, op1=ALU.mult).then_inc(s_silu, 1)

            def square(n, j):
                dve.wait_ge(s_aff, NT * n + j + 3)
                dve.wait_ge(s_core, NT * n + j + 1)
                dve.tensor_tensor(attn[j % 2][:], aff[j % 2][:], aff[j % 2][:], ALU.mult).then_inc(s_attn, 1)

            def out_norm(n):
                dve.wait_ge(s_asq, n + 1)
                link(dve.tensor_reduce(e_ss[:], osc[:], AX.X, ALU.add))
                rsqrt(link, dve, e_rn[:], e_ss[:], e_tmp[:])
                dve.tensor_tensor(e_n[:], e_ss[:], e_rn[:], ALU.mult).then_inc(s_n, 1)
                link(dve.tensor_scalar(e_rn[:], e_rn[:], 1 / NORM_EPS, None, ALU.min))

            def out_gate(n, e):
                dve.wait_ge(s_tn, n + 1)
                dve.wait_ge(s_gate, n + 1)
                link(dve.scalar_tensor_tensor(out=e_rn[:], in0=e_rn[:], scalar=hc[e][:, 1:2], in1=e_tn[:],
                                              op0=ALU.mult, op1=ALU.mult))
                link(dve.tensor_tensor(gate[e][:], gate[e][:], e_rn[:].unsqueeze(2).to_broadcast([P, NT, DV]), ALU.mult))
                dve.tensor_tensor(osc[:], agg[:], gate[e][:], ALU.mult).then_inc(s_o, 1)

            LINKS_OUT = 1 + RSQRT_LINKS + 1 + 2
            LINKS_PREP = 2 * (1 + RSQRT_LINKS + 2) + 2 * 3 + 1

            def turn(n, e, before, after, more):
                link.body(LINKS_PREP * (n + 1) + (LINKS_OUT * (n - 1) if before else 0))
                for j in range(NT):
                    if before and j == 0:
                        out_norm(n - 1)
                    if before and j == 1:
                        out_gate(n - 1, 1 - e)
                    if after:
                        if j == 1:
                            scalars(n + 1, 1 - e)
                        if j == 2:
                            norms(n + 1, 1 - e, 0)
                        if j == 3:
                            split_qk(n + 1, 0)
                            values(n + 1, 1 - e, 0)
                        if j == 4:
                            norms(n + 1, 1 - e, 1)
                        if j == 5:
                            split_qk(n + 1, 1)
                        if j == 6:
                            silu2(n + 1, 1 - e)
                        if j == 7:
                            values(n + 1, 1 - e, 1)
                    if more and j == 6:
                        weights_lo(n + 2)
                    if j < NT - 1:
                        square(n, j + 1)
                if after:
                    square(n + 1, 0)
                assert link.count == (LINKS_OUT if before else 0) + (LINKS_PREP if after else 0)

            scalars(0, 0)
            weights_lo(0)
            norms(0, 0, 0)
            split_qk(0, 0)
            values(0, 0, 0)
            norms(0, 0, 1)
            weights_lo(1)
            split_qk(0, 1)
            silu2(0, 0)
            values(0, 0, 1)
            square(0, 0)
            assert link.count == LINKS_PREP
            run_turns(dve, turn)
            link.body(LINKS_PREP * H0 + LINKS_OUT * (H0 - 1))
            out_norm(H0 - 1)
            out_gate(H0 - 1, 1)


class SplitWeights:

    BUFS = 4

    def __init__(self, st, w, src, kc, cols):
        self.w, self.src, self.kc = w, src, kc
        self.raw = [st.sb(f"wraw{i}", [P, cols]) for i in range(self.BUFS)]
        self.s_raw = [st.sem(f"sw_raw{i}") for i in range(self.BUFS)]
        self.s_hi, self.s_lo = st.sem("sw_hi"), st.sem("sw_lo")

    def load(self, sp):
        for k in range(self.kc):
            if k >= self.BUFS:
                sp.wait_ge(self.s_lo, k - self.BUFS + 1)
            sp.dma_start(self.raw[k % self.BUFS][:], self.src[:, k, :]).then_inc(self.s_raw[k % self.BUFS], 16)

    def split_hi(self, act):
        for k in range(self.kc):
            act.wait_ge(self.s_raw[k % self.BUFS], 16 * (k // self.BUFS + 1))
            act.activation(self.w[0][:, k, :], self.raw[k % self.BUFS][:], ACT.Copy).then_inc(self.s_hi, 1)

    def split_lo(self, dve):
        for k in range(self.kc):
            dve.wait_ge(self.s_hi, k + 1)
            dve.tensor_tensor(self.w[1][:, k, :], self.raw[k % self.BUFS][:], self.w[0][:, k, :].bitcast(F32),
                              ALU.subtract).then_inc(self.s_lo, 1)

    def ready(self, pe, k):
        pe.wait_ge(self.s_lo, k + 1)


class Fp4Weights:

    def __init__(self, nc, st, gu_words, gu_scales, down_words, down_scales, shift):
        self.words = {"gu": gu_words, "down": down_words.rearrange("(k w) o -> k w o", w=16)}
        self.gu_scales, self.down_scales, self.shift_dram = gu_scales, down_scales, shift
        self.raw_dt = I32
        self.loads = 2
        self.shift = st.sb("shift", [P, 1], I32)
        self.sc_gu = st.sb("sc_gu", [P, KI, KD * 2 * P], F16)
        self.sc_down = st.sb("sc_down", [P, KI, D], F16)
        self.bits = st.sb("bits", [P, KD, 2, P], I32)
        self.val = {"gu": st.sb("val_gu", [P, KD, 2, P]), "down": st.sb("val_down", [P, D])}
        self.links = 2
        self.s_const, self.const_count = st.sem("const"), 16
        self.act_scale = self.up_scale = None

    def load_constants(self, sp):
        sp.dma_start(self.shift[:], self.shift_dram).then_inc(self.s_const, 16)

    def load_gu(self, sp, raw, s_raw, i):
        sp.dma_start(raw[:].rearrange("p k a o -> p (k a o)"), self.words["gu"][i].unsqueeze(1).to_broadcast([16, 8, KD * 2 * P])).then_inc(s_raw, 16)
        sp.dma_start(self.sc_gu[:, bass.ds(i, 1), :], self.gu_scales[bass.ds(i, 1)].unsqueeze(0).to_broadcast([P, 1, KD * 2 * P])).then_inc(s_raw, 16)

    def load_down(self, sp, raw, s_raw, i):
        sp.dma_start(raw[:], self.words["down"][i].unsqueeze(1).to_broadcast([16, 8, D])).then_inc(s_raw, 16)
        sp.dma_start(self.sc_down[:, bass.ds(i, 1), :], self.down_scales[bass.ds(i, 1)].unsqueeze(0).to_broadcast([P, 1, D])).then_inc(s_raw, 16)

    def value(self, dve, link, raw, which, i, s_val):
        out = self.val[which]
        bits = self.bits[:]
        if which == "down":
            bits = bits.rearrange("p k a o -> p (k a o)")[:, 0:D]
        link(dve.tensor_scalar(bits, raw[:], self.shift[:], 19, ALU.logical_shift_left, ALU.arith_shift_right))
        link(dve.tensor_scalar(bits, bits, 0x8E00, None, ALU.bitwise_and))
        if which == "gu":
            half = bits.rearrange("p k a o -> p (k a o)").bitcast(F16).rearrange("p (o t) -> p o t", t=2)[:, :, 0]
            scale = self.sc_gu[:, bass.ds(i, 1), :].rearrange("p a o -> p (a o)")
            out = out[:].rearrange("p k a o -> p (k a o)")
        else:
            half = bits.bitcast(F16).rearrange("p (o t) -> p o t", t=2)[:, :, 0]
            scale = self.sc_down[:, bass.ds(i, 1), :].rearrange("p a o -> p (a o)")
            out = out[:]
        dve.scalar_tensor_tensor(out=out, in0=half, scalar=16384.0, in1=scale, op0=ALU.mult, op1=ALU.mult).then_inc(s_val, 1)


class PlainWeights:

    def __init__(self, nc, st, gate_t, up_t, down_t, gate_s, up_s):
        self.gate, self.up = (x.rearrange("(k p) i -> p k i", p=P) for x in (gate_t, up_t))
        self.down = down_t.rearrange("(k p) o -> k p o", p=P)
        self.scale_dram = (gate_s, up_s)
        self.raw_dt = F32
        self.loads = 2
        self.scales = st.sb("scales", [P, 2, KI])
        self.links = 0
        self.s_const, self.const_count = st.sem("const"), 32

    def load_constants(self, sp):
        for a in range(2):
            sp.dma_start(self.scales[:, a, :], self.scale_dram[a]).then_inc(self.s_const, 16)

    def load_gu(self, sp, raw, s_raw, i):
        for a, src in enumerate((self.gate, self.up)):
            sp.dma_start(raw[:, :, a, :], src[:, :, bass.ds(i * P, P)]).then_inc(s_raw, 16)

    def load_down(self, sp, raw, s_raw, i):
        sp.dma_start(raw[:], self.down[i]).then_inc(s_raw, 16)


def gate_up(nc, st, K, W):
    xT, hT, wd = K["xT"], K["hT"], K["wd"]
    fp4 = isinstance(W, Fp4Weights)
    raw_gu, raw_down = st.sb("raw_gu", [P, KD, 2, P], W.raw_dt), st.sb("raw_down", [P, D], W.raw_dt)
    w = [[st.sb(f"w{e}{part}", [P, KD, 2, P], F32R) for part in range(2)] for e in range(2)]
    sil = [st.sb(f"sil{c}", [P, 512]) for c in range(2)]
    sc = [st.sb(f"sc{e}", [P, 2]) for e in range(2)]
    gu_ps = [[st.ps(f"gu{c}{a}") for a in range(2)] for c in range(2)]
    s_rawg, s_rawd, s_valg, s_vald = st.sem("rawg"), st.sem("rawd"), st.sem("valg"), st.sem("vald")
    s_hig, s_hid, s_log, s_lod = st.sem("hig"), st.sem("hid"), st.sem("log"), st.sem("lod")
    s_mm, s_sil, s_h, s_dve, s_sc = st.sem("mm"), st.sem("sil"), st.sem("h"), st.sem("dve"), st.sem("sc")
    val_gu = W.val["gu"] if fp4 else raw_gu
    val_down = W.val["down"] if fp4 else raw_down

    def steps(step):
        with_loop = KI // 2

        def run(eng):
            with eng.Fori(0, with_loop) as h:
                step(2 * h, 0, True)
                step(2 * h + 1, 1, True)
            step(KI - 1, 0, False)
        return run

    with nc.Block() as block:
        @block.sync
        def _(sp):
            W.load_gu(sp, raw_gu, s_rawg, 0)
            W.load_constants(sp)

            def step(i, e, more):
                if more:
                    sp.wait_ge(s_valg if fp4 else s_log, i + 1)
                    W.load_gu(sp, raw_gu, s_rawg, i + 1)
                if not (isinstance(i, int) and i == 0):
                    sp.wait_ge(s_vald if fp4 else s_lod, i + 1)
                W.load_down(sp, raw_down, s_rawd, i)
            steps(step)(sp)

        @block.tensor
        def _(pe):
            pe.sem_inc(s_mm, 1)

            def step(i, e, more):
                pe.wait_ge(s_log, i + 1)
                for c in range(2):
                    pe.wait_ge(s_h, 2 * i + c + 1)
                    for a in range(2):
                        for k in range(KD):
                            for x, y in PAIRS:
                                mm = pe.matmul(gu_ps[c][a][:], w[e][y][:, k, a, :], xT[x][:, k, c * 512:(c + 1) * 512],
                                               start=(k == 0 and (x, y) == PAIRS[0]), stop=(k == KD - 1 and (x, y) == PAIRS[-1]))
                        mm.then_inc(s_mm, 1)
            steps(step)(pe)

        @block.scalar
        def _(act):
            def hi_gu(i, e):
                if fp4:
                    act.wait_ge(s_valg, i + 1)
                else:
                    act.wait_ge(s_rawg, 16 * W.loads * (i + 1))
                if not (isinstance(i, int) and i == 0):
                    act.wait_ge(s_mm, 4 * (i - 1) + 1)
                act.activation(w[e][0][:], val_gu[:], ACT.Identity).then_inc(s_hig, 1)

            def step(i, e, more):
                for c in range(2):
                    if c == 1:
                        if more:
                            hi_gu(i + 1, 1 - e)
                        if fp4:
                            act.wait_ge(s_vald, i + 2)
                        else:
                            act.wait_ge(s_rawd, 16 * (i + 1))
                        act.activation(wd[0][:, bass.ds(i, 1), :].rearrange("p a o -> p (a o)"), val_down[:], ACT.Identity).then_inc(s_hid, 1)
                    act.wait_ge(s_mm, 4 * i + 2 * c + 2)
                    act.wait_ge(s_h, 2 * i + c + 1)
                    if fp4:
                        act.activation(sil[c][:], gu_ps[c][0][:], ACT.Silu).then_inc(s_sil, 1)
                    else:
                        if c == 0:
                            act.wait_ge(s_sc, i + 1)
                        act.activation(sil[c][:], gu_ps[c][0][:], ACT.Silu, scale=sc[e][:, 0:1]).then_inc(s_sil, 1)
            hi_gu(0, 0)
            steps(step)(act)

        @block.vector
        def _(dve):
            link = Chain(dve, s_dve)
            dve.sem_inc(s_h, 2)
            dve.wait_ge(W.s_const, W.const_count)
            if fp4:
                dve.sem_inc(s_vald, 1)
            else:
                dve.sem_inc(s_lod, 1)

            def decode_gu(i):
                if fp4:
                    dve.wait_ge(s_rawg, 16 * W.loads * (i + 1))
                    W.value(dve, link, raw_gu, "gu", i, s_valg)

            def lo_gu(i, e):
                dve.wait_ge(s_hig, i + 1)
                dve.tensor_tensor(w[e][1][:], val_gu[:], w[e][0][:].bitcast(F32), ALU.subtract).then_inc(s_log, 1)
                if fp4:
                    dve.wait_ge(s_log, i + 1)

            def prep_down(i):
                if fp4:
                    dve.wait_ge(s_rawd, 16 * W.loads * (i + 1))
                    W.value(dve, link, raw_down, "down", i, s_vald)
                dve.wait_ge(s_hid, i + 1)
                at = bass.ds(i, 1)
                dve.tensor_tensor(wd[1][:, at, :].rearrange("p a o -> p (a o)"), val_down[:],
                                  wd[0][:, at, :].bitcast(F32).rearrange("p a o -> p (a o)"), ALU.subtract).then_inc(s_lod, 1)

            def product(i, e, c):
                dve.wait_ge(s_sil, 2 * i + c + 1)
                dve.wait_ge(s_mm, 4 * i + 2 * c + 3)
                dst = hT[:, bass.ds(i, 1), c * 512:(c + 1) * 512].rearrange("p a n -> p (a n)")
                dve.scalar_tensor_tensor(out=dst, in0=gu_ps[c][1][:], scalar=1.0 if fp4 else sc[e][:, 1:2], in1=sil[c][:],
                                         op0=ALU.mult, op1=ALU.mult).then_inc(s_h, 1)

            def scales(i, e):
                if not fp4:
                    if not (isinstance(i, int) and i == 0):
                        dve.wait_ge(s_h, 2 * i)
                    copy_scaled(dve, sc[e][:], W.scales[:, :, bass.ds(i, 1)].rearrange("p a o -> p (a o)")).then_inc(s_sc, 1)
                    dve.wait_ge(s_sc, i + 1)

            def step(i, e, more):
                link.body((2 * i + 1) * W.links)
                if more:
                    decode_gu(i + 1)
                product(i, e, 0)
                if more:
                    lo_gu(i + 1, 1 - e)
                    scales(i + 1, 1 - e)
                prep_down(i)
                product(i, e, 1)
                if fp4 and more:
                    dve.wait_ge(s_lod, i + 1)
            scales(0, 0)
            decode_gu(0)
            lo_gu(0, 0)
            steps(step)(dve)


def layer1_qkv(nc, st, K, src):
    w = [st.sb(f"wqkv{i}", [P, KD, C1], F32R) for i in range(2)]
    weights = SplitWeights(st, w, src.rearrange("(k p) c -> p k c", p=P), KD, C1)
    xT, qkv = K["xT"], K["qkv"]
    ps = [[st.ps(f"q{i}"), st.ps(f"kv{i}")] for i in range(2)]
    s_mm, s_q, s_kv = st.sem("mm"), st.sem("q"), st.sem("kv")
    parts = ((0, D), (D, C1))
    with nc.Block() as block:
        @block.sync
        def _(sp):
            weights.load(sp)

        @block.tensor
        def _(pe):
            for t in range(NT):
                for a, (lo, up) in enumerate(parts):
                    if t >= 2:
                        pe.wait_ge((s_q, s_kv)[a], t - 1)
                    for k in range(KD):
                        if t == 0 and a == 0:
                            weights.ready(pe, k)
                        for x, y in PAIRS:
                            mm = pe.matmul(ps[t % 2][a][:, 0:up - lo], xT[x][:, k, t * P:(t + 1) * P], w[y][:, k, lo:up],
                                           start=(k == 0 and (x, y) == PAIRS[0]), stop=(k == KD - 1 and (x, y) == PAIRS[-1]))
                    mm.then_inc(s_mm, 1)

        @block.scalar
        def _(act):
            weights.split_hi(act)
            for t in range(NT):
                act.wait_ge(s_mm, 2 * t + 1)
                act.activation(qkv[:, t, 0:D], ps[t % 2][0][:], ACT.Copy).then_inc(s_q, 1)

        @block.vector
        def _(dve):
            weights.split_lo(dve)
            for t in range(NT):
                dve.wait_ge(s_mm, 2 * t + 2)
                dve.tensor_copy(qkv[:, t, D:C1], ps[t % 2][1][:, 0:C1 - D]).then_inc(s_kv, 1)


def layer1_heads(nc, st, K):
    ident, ident_r, ident_b, mask_q, mask_k = (K[x] for x in ("ident", "ident_r", "ident_b", "mask_q", "mask_k"))
    qkv, ctx = K["qkv"], K["ctx"]
    HALF, BANKS = NT // 2, 3
    MROW = 4 * HD1
    qa = st.sb("qa", [P, NT, GS1, P], F32R)
    ka = st.sb("ka", [P, NT, P], F32R)
    va = [st.sb(f"va{e}", [P, NT, 32]) for e in range(2)]
    qt = [[st.sb(f"qt{e}{j}", [P, N], F32R) for j in range(GS1)] for e in range(2)]
    kt0 = st.sb("kt0", [P, N], F32R)
    ktm = [st.sb(f"ktm{e}", [P, N], F32R) for e in range(2)]
    ex = [[st.sb(f"ex{c}{j}", [P, 512]) for j in range(GS1)] for c in range(2)]
    mx = [st.sb(f"mx{e}", [P, NT, 2]) for e in range(2)]
    mm_ = st.sb("m", [P, NT])
    sums = st.sb("sums", [P, N])
    rden = st.sb("rden", [P, HALF, GS1])
    fill_ps = st.ps("fill")
    p1_ps = [st.ps(f"p1{i}") for i in range(BANKS)]
    p2_ps = [st.ps(f"p2{i}") for i in range(BANKS)]
    sum_ps = st.ps("sum")

    s_ka, s_qa, s_va, s_m = st.sem("ka"), st.sem("qa"), st.sem("va"), st.sem("mset")
    s_fill, s_free, s_freeo = st.sem("fill"), st.sem("free"), st.sem("freeo")
    s_p1, s_max, s_mq = st.sem("p1"), st.sem("max"), st.sem("mq")
    s_p2, s_exp, s_av, s_sum = st.sem("p2"), st.sem("exp"), st.sem("av"), st.sem("sum")
    s_dve, s_init = st.sem("dve"), st.sem("init")

    P1 = []
    for i in range(NT):
        for lo in range(0, (i + 1) * P, 512):
            used = min(512, (i + 1) * P - lo)
            P1.append((i, lo, max(used, 256), used))
    P2 = []
    for h in range(2):
        for k in range(4 * h + 4):
            first = max(0, k * P - h * 512)
            P2.append((h, k, min(first, 256), first))
    SLOTS, NP1 = len(P2), len(P1)
    STEPS, CHUNKS, FIRST1 = SLOTS * GS1, GS1 * NP1, 7
    p1_step = [FIRST1 + c * (STEPS - FIRST1 - GS1) // CHUNKS for c in range(CHUNKS)]
    FILLS = [(1, "k", 0, 0), (3, "k", 0, 1), (8, "o", 0, 0), (10, "o", 0, 1)]
    for j in range(GS1):
        start, end = p1_step[NP1 * j], p1_step[NP1 * j + NP1 - 1]
        FILLS += [(start - (2 if j == 0 else 3), "q", j, 0), (start - 1, "q", j, 1)]
        FILLS += [(min(end + 4, STEPS - 2), "m", j, 0), (min(end + 6, STEPS - 1), "m", j, 1)]
    FILLS.sort(key=lambda x: x[0])

    def fills(before, after):
        return [x for x in FILLS if (before if x[1] == "o" else after)]

    PREP_FILLS = 2 * (1 + 2 * GS1)

    def base_of(g, before):
        return PREP_FILLS * (g + 1), 2 * (g - 1) if before else 0

    def run_turns(eng, turn):
        turn(0, 0, False, True)
        with eng.Fori(0, (G1 - 2) // 2) as i:
            turn(2 * i + 1, 1, True, True)
            turn(2 * i + 2, 0, True, True)
        turn(G1 - 1, 1, True, False)

    with nc.Block() as block:
        @block.tensor
        def _(pe):
            pe.sem_inc(s_av, 2)

            def fill(g, x, state):
                _, kind, j, h = x
                if kind == "k" and h == 0:
                    pe.wait_ge(s_ka, g + 2)
                if kind == "q" and h == 0:
                    pe.wait_ge(s_qa, g + 2)
                if kind == "m" and h == 0:
                    pe.wait_ge(s_mq, GS1 * (g + 1) + j + 1)
                if kind == "o" and h == 0:
                    pe.wait_ge(s_sum, 2 * g + 1)
                if state[2] == "o":
                    pe.wait_ge(s_freeo, state[1])
                elif state[2] is not None:
                    pe.wait_ge(s_free, state[0])
                for t in range(HALF):
                    tile, cols = h * HALF + t, slice(t * P, (t + 1) * P)
                    if kind == "k":
                        tr = pe.transpose(fill_ps[:, cols].bitcast(F32R), ka[:, tile, :], ident_r[:])
                    elif kind == "o":
                        tr = pe.transpose(fill_ps[:, cols], sums[:, tile * P:(tile + 1) * P], ident[:])
                    else:
                        tr = pe.transpose(fill_ps[:, cols].bitcast(F32R), qa[:, tile, j, :], ident_r[:])
                tr.then_inc(s_fill, 1)
                state[1 if kind == "o" else 0] += 1
                state[2] = kind

            def pass1(g, e, c):
                j, (i, lo, n, used) = c // NP1, P1[c % NP1]
                at = CHUNKS * g + c
                if c % NP1 == 0:
                    pe.wait_ge(s_free, PREP_FILLS * g + FREE_AFTER["q", j])
                pe.wait_ge(s_max, at + 1)
                bank = p1_ps[c % BANKS]
                out = bank[:, 0:n]
                diag = i * P - lo
                masked = 0 <= diag < used
                mm = pe.matmul(out, qt[e][j][:, i * P:(i + 1) * P], kt0[:, lo:lo + n], start=True, stop=True)
                if masked:
                    mm = pe.matmul(bank[:, diag:diag + P], ident_b[:], mask_q[:], start=False, stop=True, skip_group_check=True)
                mm.then_inc(s_p1, 1)

            def pass2(g, e, s, j):
                h, k, lo, first = P2[s]
                at = GS1 * (SLOTS * g + s) + j
                if s == 0 and j == 0:
                    pe.wait_ge(s_free, PREP_FILLS * (g + 1))
                pe.wait_ge(s_exp, at + 1)
                bank = p2_ps[(GS1 * s + j) % BANKS]
                out = bank[:, lo:512]
                diag = k * P - h * 512
                mm = pe.matmul(out, ktm[e][:, k * P:(k + 1) * P], qt[e][j][:, h * 512 + lo:(h + 1) * 512], start=True, stop=True)
                if diag >= 0:
                    mm = pe.matmul(bank[:, diag:diag + P], ident_b[:], mask_k[:], start=False, stop=True, skip_group_check=True)
                mm.then_inc(s_p2, 1)

            def weigh(g, e, s):
                h, k, lo, first = P2[s]
                if k == 0:
                    pe.wait_ge(s_sum, 2 * g + h + 1)
                if s == 0:
                    pe.wait_ge(s_va, g + 1)
                pe.wait_ge(s_exp, GS1 * (SLOTS * g + s) + GS1 + 3)
                for j in range(GS1):
                    mm = pe.matmul(sum_ps[32 * j:32 * j + 32, first:512], va[e][:, k, :],
                                   ex[s % 2][j][:, first:512], start=(k == 0), stop=(k == 4 * h + 3))
                mm.then_inc(s_av, 1)

            FREE_AFTER, seen = {}, 0
            for f in fills(False, True):
                seen += 1
                FREE_AFTER[f[1], f[2]] = seen

            def turn(g, e, before, after):
                state = [*base_of(g, before), "m"]
                todo = fills(before, after)
                for n in range(STEPS):
                    s, j = n // GS1, n % GS1
                    for x in todo:
                        if x[0] == n:
                            fill(g, x, state)
                    pass2(g, e, s, j)
                    for c in range(CHUNKS):
                        if after and p1_step[c] == n:
                            pass1(g + 1, 1 - e, c)
                    if j == 1 and s >= 1:
                        weigh(g, e, s - 1)
                    if j == 1 and s == 0 and before:
                        weigh(g - 1, 1 - e, SLOTS - 1)

            state = [0, 0, None]
            for n in range(STEPS):
                for x in fills(False, True):
                    if x[0] == n:
                        fill(-1, x, state)
                for c in range(CHUNKS):
                    if p1_step[c] == n:
                        pass1(0, 0, c)
            run_turns(pe, turn)
            weigh(G1 - 1, 1, SLOTS - 1)
            state = [PREP_FILLS * G1, 2 * (G1 - 1), "o"]
            for h in range(2):
                fill(G1, (0, "o", 0, h), state)

        @block.scalar
        def _(act):
            act.sem_inc(s_exp, BANKS)
            act.sem_inc(s_sum, 1)

            def read_fill(n, e, x):
                _, kind, j, h = x
                act.wait_ge(s_fill, n + 1)
                cols = slice(h * 512, (h + 1) * 512)
                if kind == "k":
                    act.activation(ktm[e][:, cols], fill_ps[:], ACT.Copy)
                    act.activation(kt0[0:MROW, cols], fill_ps[0:MROW, :], ACT.Copy).then_inc(s_free, 1)
                elif kind == "q":
                    act.activation(qt[e][j][0:MROW, cols], fill_ps[0:MROW, :], ACT.Copy).then_inc(s_free, 1)
                else:
                    act.activation(qt[e][j][MROW:MROW + 32, cols], fill_ps[MROW:MROW + 32, :], ACT.Copy).then_inc(s_free, 1)

            def exps(g, s, j):
                h, k, lo, first = P2[s]
                at = GS1 * (SLOTS * g + s) + j
                act.wait_ge(s_p2, at + 1)
                act.wait_ge(s_av, SLOTS * g + s + 1)
                act.activation(ex[s % 2][j][:, first:512], p2_ps[(GS1 * s + j) % BANKS][:, first:512], ACT.Exp, scale=HD1 ** -0.5).then_inc(s_exp, 1)

            def sums_out(g, h):
                act.wait_ge(s_av, SLOTS * g + (HALF if h == 0 else SLOTS) + 2)
                act.activation(sums[:, h * 512:(h + 1) * 512], sum_ps[:], ACT.Copy).then_inc(s_sum, 1)

            def turn(g, e, before, after):
                a, o = base_of(g, before)
                filled = a + o
                todo = fills(before, after)
                for n in range(STEPS):
                    s, j = n // GS1, n % GS1
                    for x in todo:
                        if x[0] == n:
                            if x[1] != "o":
                                read_fill(filled, 1 - e, x)
                            filled = filled + 1
                    if before and n == 3:
                        sums_out(g - 1, 1)
                    if n == GS1 * HALF + 3:
                        sums_out(g, 0)
                    exps(g, s, j)

            act.wait_ge(s_init, 1 + 2 * GS1)
            for n, x in enumerate(fills(False, True)):
                read_fill(n, 0, x)
            run_turns(act, turn)
            sums_out(G1 - 1, 1)

        @block.gpsimd
        def _(pool):
            pool.memset(kt0[MROW:P, :].bitcast(F32), 0.0).then_inc(s_init, 1)
            for e in range(2):
                for j in range(GS1):
                    pool.memset(qt[e][j][MROW:P, :].bitcast(F32), 0.0).then_inc(s_init, 1)

        @block.vector
        def _(dve):
            link = Chain(dve, s_dve)
            dve.sem_inc(s_max, BANKS)
            for x in (ka[:].rearrange("p t c -> p (t c)"), qa[:].rearrange("p t g c -> p (t g c)")):
                link(dve.memset(x.bitcast(F32), 0.0))
            link(dve.memset(ka[:, :, MROW:MROW + 2].bitcast(F32), -1.0))
            for e in range(2):
                link(dve.memset(va[e][:], 0.0))
                link(dve.memset(va[e][:, :, HD1:HD1 + 1], 1.0))
                link(dve.memset(mx[e][:], -3.0e38))
            SETUP = link.count

            def build(g, e, n):
                if n is not None:
                    dve.wait_ge(s_fill, n)
                ks = qkv[:, :, bass.ds(D + g * HD1, HD1)]
                vs = qkv[:, :, bass.ds(D + G1 * HD1 + g * HD1, HD1)]
                qs = qkv[:, :, bass.ds(g * GS1 * HD1, GS1 * HD1)].rearrange("p t (j d) -> p t j d", j=GS1)
                part = [slice(i * HD1, (i + 1) * HD1) for i in range(4)]
                link(copy_scaled(dve, ka[:, :, part[0]], ks))
                link(copy_scaled(dve, ka[:, :, part[1]], ks))
                link(dve.tensor_tensor(ka[:, :, part[2]], ks, ka[:, :, part[0]].bitcast(F32), ALU.subtract))
                dve.tensor_tensor(ka[:, :, part[3]], ks, ka[:, :, part[0]].bitcast(F32), ALU.subtract).then_inc(s_ka, 1)
                link(copy_scaled(dve, qa[:, :, :, part[0]], qs))
                link(copy_scaled(dve, qa[:, :, :, part[2]], qs))
                link(dve.tensor_tensor(qa[:, :, :, part[1]], qs, qa[:, :, :, part[0]].bitcast(F32), ALU.subtract))
                dve.tensor_tensor(qa[:, :, :, part[3]], qs, qa[:, :, :, part[0]].bitcast(F32), ALU.subtract).then_inc(s_qa, 1)
                if n is not None:
                    dve.wait_ge(s_av, SLOTS * (g - 1) + 2)
                copy_scaled(dve, va[e][:, :, 0:HD1], vs).then_inc(s_va, 1)
            LINKS_BUILD = 6

            def maxima(g, c):
                j, (i, lo, n, used) = c // NP1, P1[c % NP1]
                at = CHUNKS * g + c
                dve.wait_ge(s_p1, at + 1)
                dve.tensor_reduce(mx[j % 2][:, i, lo // 512:lo // 512 + 1], p1_ps[c % BANKS][:, 0:used], AX.X, ALU.max).then_inc(s_max, 1)
                if c % NP1 == NP1 - 1:
                    dve.wait_ge(s_max, at + 1 + BANKS)
                    link(dve.tensor_tensor(mm_[:], mx[j % 2][:, :, 0], mx[j % 2][:, :, 1], ALU.max))
                    link(dve.tensor_copy(qa[:, :, j, MROW], mm_[:]))
                    dve.tensor_tensor(qa[:, :, j, MROW + 1], mm_[:], qa[:, :, j, MROW].bitcast(F32), ALU.subtract).then_inc(s_mq, 1)
                    dve.wait_ge(s_mq, GS1 * g + j + 1)
            LINKS_MAX = 2 * GS1

            def output(g, h, n):
                dve.wait_ge(s_fill, n + 1)
                x = fill_ps[:].rearrange("p (t j c) -> p t j c", t=HALF, j=GS1)
                link(dve.reciprocal(rden[:], x[:, :, :, HD1]))
                dst = ctx[:, h * HALF:(h + 1) * HALF, bass.ds(g * GS1 * HD1, GS1 * HD1)].rearrange("p t (j d) -> p t j d", j=GS1)
                dve.tensor_tensor(dst, x[:, :, :, 0:HD1], rden[:].unsqueeze(3).to_broadcast([P, HALF, GS1, HD1]), ALU.mult).then_inc(s_freeo, 1)
                dve.wait_ge(s_freeo, 2 * g + h + 1)
            LINKS_OUT = 2

            def turn(g, e, before, after):
                a, o = base_of(g, before)
                n = a + o
                link.body(SETUP + (LINKS_BUILD + LINKS_MAX) * (g + 1) + (LINKS_OUT * (g - 1) if before else 0))
                if after:
                    build(g + 1, 1 - e, n)
                todo = fills(before, after)
                for step in range(STEPS):
                    for x in todo:
                        if x[0] == step:
                            if x[1] == "o":
                                output(g - 1, x[3], n)
                            n = n + 1
                    for c in range(CHUNKS):
                        if after and p1_step[c] == step:
                            maxima(g + 1, c)

            build(0, 0, None)
            for c in range(CHUNKS):
                maxima(0, c)
            run_turns(dve, turn)
            link.body(SETUP + (LINKS_BUILD + LINKS_MAX) * G1 + LINKS_OUT * (G1 - 1))
            for h in range(2):
                output(G1 - 1, h, PREP_FILLS * G1 + 2 * (G1 - 1) + h)


class TransposeCtx:

    def __init__(self, st, K):
        self.ctx, self.cT, self.ident = K["ctx"], K["cT"], K["ident"]
        self.ps = [st.ps(f"t{i}") for i in range(2)]
        self.s_tr, self.s_rd = st.sem("ctx_tr"), st.sem("ctx_rd")

    def transposes(self, pe):
        for t in range(NT):
            if t >= 2:
                pe.wait_ge(self.s_rd, t - 1)
            for k in range(KD):
                tr = pe.transpose(self.ps[t % 2][:, k * P:(k + 1) * P], self.ctx[:, t, k * P:(k + 1) * P], self.ident[:])
            tr.then_inc(self.s_tr, 1)

    def copies(self, act):
        for t in range(NT):
            act.wait_ge(self.s_tr, t + 1)
            act.activation(self.cT[:, :, t * P:(t + 1) * P], self.ps[t % 2][:].rearrange("p (k n) -> p k n", k=KD), ACT.Copy).then_inc(self.s_rd, 1)
        act.wait_ge(self.s_rd, NT)


def program(nc, T, out, stages=99):
    ctx = ExitStack()
    with ctx:
        def sb(name, shape, dt=F32):
            return ctx.enter_context(nc.sbuf_tensor(name, shape, dt))

        K = {"ident": sb("ident", [P, P]), "ident_r": sb("ident_r", [P, P], F32R), "ident_b": sb("ident_b", [P, P], BF16),
             "mask_q": sb("mask_q", [P, P], BF16), "mask_k": sb("mask_k", [P, P], BF16), "scal": sb("scal", [P, 3, H0]),
             "ls_iaw": T["ls_iaw"], "ls_hws": T["ls_hws"],
             "xT": [sb("xT_hi", [P, KD, N], F32R), sb("xT_lo", [P, KD, N], F32R)]}
        with Stage(nc, "const") as st:
            constants(nc, st, K)
        mid = [nc.dram_tensor(f"mid{i}", (B, N, D), F32, kind="Internal").ap().rearrange("b (t p) d -> b t p d", p=P) for i in range(3)]
        x0, x4 = (x.rearrange("b (t p) d -> b t p d", p=P) for x in (T["tokens"], out))
        with nc.Fori(0, B) as b:
            def held(c, name, shape, dt=F32):
                K[name] = c.enter_context(nc.sbuf_tensor(f"{name}_{layer}", shape, dt))

            def tile_of(x):
                return lambda t: x[b, t]

            layer = 0
            with Stage(nc, "in") as st:
                finish_tokens(nc, st, K, tile_of(x0), None)
            with ExitStack() as c:
                held(c, "oT", [P, H0, N])
                with Stage(nc, "heads0") as st:
                    layer0_heads(nc, st, K, T["Wqg"], T["Wkv"])
                with Stage(nc, "out0") as st:
                    w = [st.sb(f"wo{i}", [P, H0, D], F32R) for i in range(2)]
                    finish_tokens(nc, st, K, tile_of(x0), tile_of(mid[0]), kc=H0, src=K["oT"], w=w,
                                  weights=SplitWeights(st, w, T["Wo0"].rearrange("(k p) c -> p k c", p=P), H0, D))
            for layer in range(2):
                if layer == 1:
                    with ExitStack() as c:
                        held(c, "ctx", [P, NT, D])
                        held(c, "qkv", [P, NT, C1])
                        with Stage(nc, "qkv1") as st:
                            layer1_qkv(nc, st, K, T["Wqkv1"])
                        with Stage(nc, "heads1") as st:
                            layer1_heads(nc, st, K)
                        held(c, "cT", [P, KD, N])
                        with Stage(nc, "out1") as st:
                            w = [st.sb(f"wo{i}", [P, KD, D], F32R) for i in range(2)]
                            finish_tokens(nc, st, K, tile_of(mid[1]), tile_of(mid[2]), kc=KD, src=K["cT"], w=w,
                                          weights=SplitWeights(st, w, T["Wo1"].rearrange("(k p) c -> p k c", p=P), KD, D),
                                          transpose=TransposeCtx(st, K))
                with ExitStack() as c:
                    held(c, "hT", [P, KI, N])
                    K["wd"] = [c.enter_context(nc.sbuf_tensor(f"wd{i}_{layer}", [P, KI, D], F32R)) for i in range(2)]
                    with Stage(nc, f"gu{layer}") as st:
                        if layer == 0:
                            W = Fp4Weights(nc, st, T["gu_words"], T["gu_scales"], T["down_words"], T["down_scales"], T["shift"])
                        else:
                            W = PlainWeights(nc, st, T["gate1"], T["up1"], T["down1"], T["gate_s"], T["up_s"])
                        gate_up(nc, st, K, W)
                    with Stage(nc, f"down{layer}") as st:
                        if layer == 0:
                            finish_tokens(nc, st, K, tile_of(mid[0]), tile_of(mid[1]), kc=KI, src=K["hT"], w=K["wd"], norm="rms")
                        else:
                            ds = st.sb("down_s", [P, D])
                            s_ds = st.sem("ds")
                            finish_tokens(nc, st, K, tile_of(mid[2]), tile_of(x4), kc=KI, src=K["hT"], w=K["wd"],
                                          y_scale=(ds, T["down_s"], s_ds), more=False)


_IN = ["tokens", "Wqg", "Wkv", "Wo0", "ls_iaw", "ls_hws", "gu_words", "gu_scales", "down_words", "down_scales", "shift",
       "Wqkv1", "Wo1", "gate1", "up1", "down1", "gate_s", "up_s", "down_s"]


def layout(i):
    import numpy as np

    c = np.ascontiguousarray
    return {
        "tokens": i["L0_attn_tokens"], "Wqg": i["L0_attn_Wqg"], "Wkv": i["L0_attn_Wkv"], "Wo0": i["L0_attn_Wo"],
        "ls_iaw": i["L0_attn_ls_iaw"], "ls_hws": i["L0_attn_ls_hws"],
        "gu_words": c(i["L0_ffn_gate_up_packed"].T.reshape(KD, 16, 2, KI, P).transpose(3, 1, 0, 2, 4)).reshape(KI, 16, KD * 2 * P),
        "gu_scales": c(i["L0_ffn_gate_up_scales"].reshape(KD, 2, KI, P).transpose(2, 0, 1, 3)).reshape(KI, KD * 2 * P),
        "down_words": c(i["L0_ffn_down_packed"].T), "down_scales": i["L0_ffn_down_scales"],
        "shift": np.array([[28 - 4 * (p % 8)] for p in range(P)], np.int32),
        "Wqkv1": c(np.concatenate([i["L1_attn_Wq"], i["L1_attn_Wk"], i["L1_attn_Wv"]], axis=0).T),
        "Wo1": c(i["L1_attn_Wo"].T), "gate1": c(i["L1_ffn_gate_w"].T), "up1": c(i["L1_ffn_up_w"].T),
        "down1": c(i["L1_ffn_down_w"].T), "gate_s": c(i["L1_ffn_gate_s"].reshape(KI, P).T), "up_s": c(i["L1_ffn_up_s"].reshape(KI, P).T), "down_s": i["L1_ffn_down_s"],
    }


def kernel(**inputs):
    import numpy as np
    import concourse.bacc as bacc
    from concourse.bass_utils import run_bass_kernel_spmd

    nc = bacc.Bacc("TRN2", target_bir_lowering=False, num_devices=1)
    arrays = layout({k: np.asarray(v) for k, v in inputs.items()})
    T = {k: nc.dram_tensor(f"in_{k}", arrays[k].shape, mybir.dt.from_np(arrays[k].dtype), kind="ExternalInput").ap() for k in _IN}
    out = nc.dram_tensor("out_x", (B, N, D), F32, kind="ExternalOutput").ap()
    program(nc, T, out)
    r = run_bass_kernel_spmd(nc, [{f"in_{k}": arrays[k] for k in _IN}], core_ids=[0])
    return r.results[0]["out_x"]
```
